# Optimizing a Trainium2 kernel written in Bass

```python
import numpy as np
import jax
import jax.numpy as jnp

def _softmax(x, axis=-1):
    return jax.nn.softmax(x, axis=axis)

def _gelu(x):
    return jax.nn.gelu(x, approximate=True)

def _silu(x):
    return jax.nn.silu(x)

def _sigmoid(x):
    return jax.nn.sigmoid(x)

def _layernorm(x, axis=-1, eps=1e-05):
    m = jnp.mean(x, axis=axis, keepdims=True)
    v = jnp.var(x, axis=axis, keepdims=True)
    return (x - m) / jnp.sqrt(v + eps)

def _scatter_add(tgt, idx, src, axis=0):
    return tgt.at[idx].add(src)

def _segment_sum(src, seg, n):
    return jax.ops.segment_sum(src, seg, n)
kernel_name = 'mk_seq_postln_d1_jaxref_r4_9f0d09'

def setup_inputs(seed: int=0):
    np.random.seed(seed)
    _w = jnp.asarray

    def _L0_attn_setup():
        import jax, jax.numpy as jnp
        import numpy as np
        NUM_HEADS = 16
        LORA_SCALE = 32.0 / 8.0
        ROPE_BASE = 10000.0

        def make_sincos(seq_len, dim):
            pos = jnp.arange(seq_len, dtype=jnp.float32)
            i = jnp.arange(0, dim, 2, dtype=jnp.float32) / dim
            theta = pos[:, None] / ROPE_BASE ** i[None, :]
            return (jnp.sin(theta), jnp.cos(theta))

        def apply_rope(x, sin, cos):
            x_even = x[..., 0::2]
            x_odd = x[..., 1::2]
            rot_even = x_even * cos - x_odd * sin
            rot_odd = x_even * sin + x_odd * cos
            return jnp.stack([rot_even, rot_odd], axis=-1).reshape(x.shape)
        key = jax.random.key(seed)
        ks = jax.random.split(key, 9)
        B, T, D, R = (4, 512, 256, 8)
        s = 1.0 / np.sqrt(D)
        return {'query': jax.random.normal(ks[0], (B, T, D), dtype=jnp.float32), 'wq': jax.random.normal(ks[1], (D, D), dtype=jnp.float32) * s, 'wk': jax.random.normal(ks[2], (D, D), dtype=jnp.float32) * s, 'wv': jax.random.normal(ks[3], (D, D), dtype=jnp.float32) * s, 'wo': jax.random.normal(ks[4], (D, D), dtype=jnp.float32) * s, 'Aq': jax.random.normal(ks[5], (D, R), dtype=jnp.float32) * s, 'Bq': jax.random.normal(ks[6], (R, D), dtype=jnp.float32) * 0.01, 'Av': jax.random.normal(ks[7], (D, R), dtype=jnp.float32) * s, 'Bv': jax.random.normal(ks[8], (R, D), dtype=jnp.float32) * 0.01}
    _L0_attn_in = _L0_attn_setup()

    def _L0_ffn_setup():
        import jax, jax.numpy as jnp
        import numpy as np
        D_MODEL = 256
        EXPANSION = 4
        D_HIDDEN = D_MODEL * EXPANSION
        NUM_STAGES = int(np.log2(D_HIDDEN))

        def butterfly(y, weights, dim):
            lead = y.shape[:-1]
            for stage in range(weights.shape[0]):
                s = 2 ** stage
                nb = dim // (2 * s)
                yr = y.reshape(*lead, nb, 2, s)
                a = yr[..., 0, :]
                b = yr[..., 1, :]
                w = weights[stage].reshape(nb, s, 2, 2)
                na = w[..., 0, 0] * a + w[..., 0, 1] * b
                nb2 = w[..., 1, 0] * a + w[..., 1, 1] * b
                y = jnp.stack([na, nb2], axis=-2).reshape(*lead, dim)
            return y
        key = jax.random.key(seed)
        ks = jax.random.split(key, 6)
        B, S = (4, 512)
        x = jax.random.normal(ks[0], (B, S, D_MODEL), jnp.float32)
        W_exp = jax.random.normal(ks[1], (D_MODEL, D_HIDDEN), jnp.float32) * 0.02
        b_exp = jnp.zeros((D_HIDDEN,), jnp.float32)
        up_weights = jax.random.normal(ks[2], (NUM_STAGES, D_HIDDEN // 2, 2, 2), jnp.float32) * 0.02
        up_bias = jnp.zeros((D_HIDDEN,), jnp.float32)
        down_weights = jax.random.normal(ks[3], (NUM_STAGES, D_HIDDEN // 2, 2, 2), jnp.float32) * 0.02
        W_con = jax.random.normal(ks[4], (D_HIDDEN, D_MODEL), jnp.float32) * 0.02
        b_con = jnp.zeros((D_MODEL,), jnp.float32)
        down_bias = jnp.zeros((D_MODEL,), jnp.float32)
        return dict(x=x, W_exp=W_exp, b_exp=b_exp, up_weights=up_weights, up_bias=up_bias, down_weights=down_weights, W_con=W_con, b_con=b_con, down_bias=down_bias)
    _L0_ffn_in = _L0_ffn_setup()
    _d = {'L0_attn_query': _L0_attn_in['query'], 'L0_attn_wq': _L0_attn_in['wq'], 'L0_attn_wk': _L0_attn_in['wk'], 'L0_attn_wv': _L0_attn_in['wv'], 'L0_attn_wo': _L0_attn_in['wo'], 'L0_attn_Aq': _L0_attn_in['Aq'], 'L0_attn_Bq': _L0_attn_in['Bq'], 'L0_attn_Av': _L0_attn_in['Av'], 'L0_attn_Bv': _L0_attn_in['Bv'], 'L0_ffn_W_exp': _L0_ffn_in['W_exp'], 'L0_ffn_b_exp': _L0_ffn_in['b_exp'], 'L0_ffn_up_weights': _L0_ffn_in['up_weights'], 'L0_ffn_up_bias': _L0_ffn_in['up_bias'], 'L0_ffn_down_weights': _L0_ffn_in['down_weights'], 'L0_ffn_W_con': _L0_ffn_in['W_con'], 'L0_ffn_b_con': _L0_ffn_in['b_con'], 'L0_ffn_down_bias': _L0_ffn_in['down_bias']}
    _x0 = _d['L0_attn_query']
    _d['L0_attn_query'] = jax.random.normal(jax.random.fold_in(jax.random.key(seed), 1), (16, 512, 256), dtype=_x0.dtype)
    del _x0
    return _d

def reference(L0_attn_query, L0_attn_wq, L0_attn_wk, L0_attn_wv, L0_attn_wo, L0_attn_Aq, L0_attn_Bq, L0_attn_Av, L0_attn_Bv, L0_ffn_W_exp, L0_ffn_b_exp, L0_ffn_up_weights, L0_ffn_up_bias, L0_ffn_down_weights, L0_ffn_W_con, L0_ffn_b_con, L0_ffn_down_bias):

    def _L0_attn_ref(query, wq, wk, wv, wo, Aq, Bq, Av, Bv):
        import jax, jax.numpy as jnp
        import numpy as np
        NUM_HEADS = 16
        LORA_SCALE = 32.0 / 8.0
        ROPE_BASE = 10000.0

        def make_sincos(seq_len, dim):
            pos = jnp.arange(seq_len, dtype=jnp.float32)
            i = jnp.arange(0, dim, 2, dtype=jnp.float32) / dim
            theta = pos[:, None] / ROPE_BASE ** i[None, :]
            return (jnp.sin(theta), jnp.cos(theta))

        def apply_rope(x, sin, cos):
            x_even = x[..., 0::2]
            x_odd = x[..., 1::2]
            rot_even = x_even * cos - x_odd * sin
            rot_odd = x_even * sin + x_odd * cos
            return jnp.stack([rot_even, rot_odd], axis=-1).reshape(x.shape)
        B, T, D = query.shape
        H = NUM_HEADS
        dh = D // H
        q = query @ wq + query @ Aq @ Bq * LORA_SCALE
        k = query @ wk
        v = query @ wv + query @ Av @ Bv * LORA_SCALE

        def split(x):
            return x.reshape(B, T, H, dh).transpose(0, 2, 1, 3)
        q, k, v = (split(q), split(k), split(v))
        sin, cos = make_sincos(T, dh)
        q = apply_rope(q, sin, cos)
        k = apply_rope(k, sin, cos)
        scores = jnp.einsum('bhqd,bhkd->bhqk', q, k) / jnp.sqrt(jnp.float32(dh))
        causal = jnp.triu(jnp.ones((T, T), dtype=bool), k=1)
        scores = jnp.where(causal[None, None], jnp.float32(-1000000000.0), scores)
        attn = jax.nn.softmax(scores, axis=-1)
        out = jnp.einsum('bhqk,bhkd->bhqd', attn, v)
        out = out.transpose(0, 2, 1, 3).reshape(B, T, D)
        return out @ wo

    def _L0_ffn_ref(x, W_exp, b_exp, up_weights, up_bias, down_weights, W_con, b_con, down_bias):
        import jax, jax.numpy as jnp
        import numpy as np
        D_MODEL = 256
        EXPANSION = 4
        D_HIDDEN = D_MODEL * EXPANSION
        NUM_STAGES = int(np.log2(D_HIDDEN))

        def butterfly(y, weights, dim):
            lead = y.shape[:-1]
            for stage in range(weights.shape[0]):
                s = 2 ** stage
                nb = dim // (2 * s)
                yr = y.reshape(*lead, nb, 2, s)
                a = yr[..., 0, :]
                b = yr[..., 1, :]
                w = weights[stage].reshape(nb, s, 2, 2)
                na = w[..., 0, 0] * a + w[..., 0, 1] * b
                nb2 = w[..., 1, 0] * a + w[..., 1, 1] * b
                y = jnp.stack([na, nb2], axis=-2).reshape(*lead, dim)
            return y
        h = jnp.einsum('bsd,dh->bsh', x, W_exp) + b_exp
        h = butterfly(h, up_weights, D_HIDDEN)
        h = jax.nn.gelu(h + up_bias, approximate=False)
        h = butterfly(h, down_weights, D_HIDDEN)
        y = jnp.einsum('bsh,hd->bsd', h, W_con) + b_con
        return y + down_bias
    x = L0_attn_query
    x = _layernorm(x + _L0_attn_ref(x, L0_attn_wq, L0_attn_wk, L0_attn_wv, L0_attn_wo, L0_attn_Aq, L0_attn_Bq, L0_attn_Av, L0_attn_Bv), axis=-1)
    x = _layernorm(x + _L0_ffn_ref(x, L0_ffn_W_exp, L0_ffn_b_exp, L0_ffn_up_weights, L0_ffn_up_bias, L0_ffn_down_weights, L0_ffn_W_con, L0_ffn_b_con, L0_ffn_down_bias), axis=-1)
    return x

_drawn_inputs = setup_inputs


def setup_inputs(seed=0):
    import zlib

    import numpy as np

    out = dict(_drawn_inputs(seed))
    spreads = {'L0_ffn_b_exp': (0.0, 0.1),
     'L0_ffn_up_bias': (0.0, 0.1),
     'L0_ffn_b_con': (0.0, 0.1),
     'L0_ffn_down_bias': (0.0, 0.1)}
    factors = {'L0_attn_Aq': 3.421, 'L0_attn_Bq': 3.472, 'L0_attn_Av': 3.265, 'L0_attn_Bv': 3.17}
    for name, (base, spread) in spreads.items():
        noise = np.random.default_rng([zlib.crc32(name.encode()), seed]).standard_normal(out[name].shape)
        drawn = base * np.exp(spread * noise) if base else spread * noise
        out[name] = jnp.asarray(drawn.astype(out[name].dtype))
    for name, factor in factors.items():
        out[name] = (out[name] * factor).astype(out[name].dtype)
    return out
```

```python
import concourse.bass as bass
from concourse import mybir
from contextlib import ExitStack

FP32 = mybir.dt.float32
BF16 = mybir.dt.bfloat16
ALU = mybir.AluOpType
ACT = mybir.ActivationFunctionType
AX = mybir.AxisListType

B, T, D = 16, 512, 256
H, DH = 16, 16
HID = 1024
P = 128
NT = T // P
KD = D // P
NHT = HID // P
GH = 4
NG = H // GH
UG = 5
NU = NG * UG
LEAD = 8
R = 8
NPART = 3
PRODUCTS = [(0, 0), (1, 0), (2, 0), (0, 1), (1, 1), (0, 2)]
NK = len(PRODUCTS) * DH
EPS = 1e-5
LORA = 4.0
SCALE = 0.25
STAGES_IN = 7
STAGES_X = 3
NPAIR = HID // 2
DMA = 16


def pos(tile):
    return (tile + NT - 1) % NT


def steps(i, static):
    out = []

    def put(kind, b, n=0, top=B):
        if not static or 0 <= b < top:
            out.append((kind, b, n))

    for t in range(NU):
        g, u = t // UG, t % UG
        if t == 0:
            put("OE", i - 1, 2)
            put("RAW", i - 1, 2)
            put("FILL", i, 3)
            put("XRES", i - 1)
        if t == 5:
            put("OE", i - 1, 3)
            put("VC", i)
            put("RAW", i - 1, 3)
            put("FILL", i + 1, 0)
        if t == 10:
            put("OE", i, 0)
            put("RAW", i, 0)
            put("FILL", i + 1, 1)
        if t == 15:
            put("OE", i, 1)
            put("RAW", i, 1)
            put("FILL", i + 1, 2)
        put("ST", i, t)
        first = {0: ("QK", i + 1, 0), 1: ("QK", i + 1, 2), 2: ("MT", i, 1), 6: ("V", i + 1, 0), 8: ("V", i + 1, 1),
                 7: ("MT", i, 2), 10: ("WO", i - 1, 0), 12: ("MT", i, 3), 13: ("XT", i - 1, 1),
                 14: ("W1", i - 1, 1), 15: ("W1", i - 1, 3), 16: ("W1", i - 1, 5),
                 17: ("MT", i + 1, 0), 19: ("W2", i - 1, 0)}
        if t in first:
            put(*first[t])
        if t + LEAD < NU:
            put("S", i, t + LEAD)
        else:
            put("S", i + 1, t + LEAD - NU)
        if t == 1:
            put("SPLIT", i + 1, 0)
        if u >= 1:
            if g == 0:
                put("PV", i - 1, 4 * (NG - 1) + u - 1)
            else:
                put("PV", i, 4 * (g - 1) + u - 1)
        second = {0: ("QK", i + 1, 1), 1: ("QK", i + 1, 3),
                  10: ("WO", i - 1, 1), 12: ("XT", i - 1, 0), 13: ("W1", i - 1, 0),
                  14: ("W1", i - 1, 2), 15: ("W1", i - 1, 4), 16: ("W1", i - 1, 6),
                  17: ("W1", i - 1, 7), 19: ("W2", i - 1, 1)}
        if t in second:
            put(*second[t])
        if t == 0:
            put("ROPE", i + 1, 0)
        if t == 1:
            put("ROPE", i + 1, 1)
        if t == 2:
            put("SPLIT", i + 1, 1)
            put("MROW", i, 1)
            put("QKW", i + 1, 0)
            put("QKW", i + 1, 1)
        if t == 9:
            put("XTL", i + 2, 0, B + 1)
        if t == 6:
            put("SMOC", i - 1, 1)
        if t == 7:
            put("MROW", i, 2)
            put("RCP", i - 1, 1)
            put("REC", i - 1, 1)
            put("ON", i - 1, 1)
        if t == 10:
            put("LNA", i - 1, 0)
        if t == 11:
            put("LNB", i - 1, 0)
        if t == 12:
            put("MROW", i, 3)
        if t == 16:
            put("SMOC", i, 0)
            put("GE", i - 1, 0)
        if t == 17:
            put("MROW", i + 1, 0)
            put("RCP", i, 0)
            put("REC", i, 0)
        if t == 18:
            put("GE", i - 1, 1)
            put("ON", i, 0)
        if t == 19:
            put("LNA", i - 1, 1)
            put("LNB", i - 1, 1)
            put("OUT", i - 1)
    return out


MISC = ("QK", "V", "MT", "WO", "XT", "W1", "W2")
PER = {"QK": 4, "V": 2, "MT": 4, "WO": 2, "XT": 2, "W1": NHT, "W2": 2}


def layer(nc, xT_d, x_d, wqk_d, wv_d, aqT_d, bq_d, avT_d, bv_d, wo_d, wexpT_d, bexp_d, upin_d,
          upx_d, upbias_d, dnin_d, dnx_d, wcon_d, bcon_d, dbias_d, cos_d, sin_d, ident_d, mask_d,
          out_d):
    ctx = ExitStack()
    with ctx:
        def sb(name, shape, dt=FP32):
            return ctx.enter_context(nc.sbuf_tensor(name, shape, dt))

        def pb(name, shape, dt=FP32):
            return ctx.enter_context(nc.psum_tensor(name, shape, dt))

        def sem(name):
            return ctx.enter_context(nc.semaphore(name))

        q_st = sb("q_st", [P, H, T], BF16)
        k_st = sb("k_st", [P, H, T], BF16)
        pT = sb("pT", [P, 2, UG, 2 * T])
        xT = sb("xT", [P, KD, T])
        cosT = sb("cosT", [P, T])
        sinT = sb("sinT", [P, T])
        rope_in = sb("rope_in", [P, 4, T])
        rot = sb("rot", [P, 2, T])
        parts = sb("parts", [P, 2, NPART, 2, T], BF16)
        v_new = sb("v_new", [P, NT, D])
        v_aug = sb("v_aug", [P, NT, H, 2 * DH])
        o_raw = sb("o_raw", [P, T])
        o_c = sb("o_c", [P, 2, T])
        r_b = sb("r_b", [P, 2, T])
        s_m = sb("s_m", [64, 64])
        r_m = sb("r_m", [64, 64])
        x_res = sb("x_res", [P, NT, D])
        x1 = sb("x1", [P, NT, D])
        x1T = sb("x1T", [P, KD, T])
        gact = sb("gact", [P, NHT, T])
        y = sb("y", [P, NT, D])
        m_raw = sb("m_raw", [P, NT, GH])
        m_res = sb("m_res", [P, NT, GH])
        m_part = sb("m_part", [P, NT, NPART, GH], BF16)
        m_row = sb("m_row", [NPART * GH, T], BF16)
        wqk = sb("wqk", [P, KD, 4 * P])
        wv = sb("wv", [P, KD, D])
        wo = sb("wo", [P, KD, D])
        w1 = sb("w1", [P, KD, HID])
        w2 = sb("w2", [P, NHT, D])
        bias_out = sb("bias_out", [P, D])
        gbias = sb("gbias", [P, NHT])
        ident = sb("ident", [P, P])
        identb = sb("identb", [P, P], BF16)
        maskb = sb("maskb", [P, 2 * P], BF16)
        stats = sb("stats", [P, 2, NT, 6])
        mv = sb("mv", [P, 2, NT, 2])
        ve = sb("ve", [P, 2, NT])
        rstd = sb("rstd", [P, 2, NT])
        mhalf = sb("mhalf", [P, NT])
        lora_a = sb("lora_a", [R, 2, D])
        lora_b = sb("lora_b", [R, 2, D])
        w_x = sb("w_x", [P, 2, STAGES_X, 4, 4])
        pT_flat = pT[:, :, :, :].rearrange("p a u c -> p (a u c)")
        mat = [[pT_flat[:, (2 * k + j) * HID:(2 * k + j + 1) * HID] for j in range(2)]
               for k in range(2)]
        win = [pT_flat[:, (4 + 2 * k) * HID:(6 + 2 * k) * HID] for k in range(2)]
        wide = 2 * (D + 1) * 4
        tup = [gact[:, :, 0:D + 1], gact[:, :, D + 1:2 * D].rearrange("p a b -> p a b")]
        q32 = q_st[:, :, :].rearrange("p h t -> p (h t)").bitcast(FP32)
        k32 = k_st[:, :, :].rearrange("p h t -> p (h t)").bitcast(FP32)
        tup = [q32[:, 0:NHT * (D + 1)].rearrange("p (b c) -> p b c", b=NHT),
               k32[:, 0:NHT * (D + 1)].rearrange("p (b c) -> p b c", b=NHT)]
        tdn = [gact[:, 0:4, :].rearrange("p a c -> p (a c)").rearrange("p (b c) -> p b c", b=NHT),
               gact[:, 4:8, :].rearrange("p a c -> p (a c)").rearrange("p (b c) -> p b c", b=NHT)]
        tmp_v = x1[:, :, :].rearrange("p a c -> p (a c)")
        tmp_p = x1T[:, :, :].rearrange("p a c -> p (a c)")
        tmp_x = y[:, 0:2, :].rearrange("p a c -> p (a c)")

        ps_t = pb("ps_t", [P, 2, 2 * T])
        ps_s = pb("ps_s", [P, 2 * T])
        ps_o = pb("ps_o", [P, T])
        ps_m = pb("ps_m", [P, T])
        ps_mb = ps_m[:, :].bitcast(BF16)

        qk_scr = nc.dram_tensor("qk_scr", (B, 2, NPART * DH, H, T), BF16, kind="Internal").ap()
        o_scr = nc.dram_tensor("o_scr", (B, NG, P, T), FP32, kind="Internal").ap()
        m_scr = nc.dram_tensor("m_scr", (B, NG, NPART * GH, T), BF16, kind="Internal").ap()
        r_scr = nc.dram_tensor("r_scr", (B, 2, 8, T), FP32, kind="Internal").ap()

        xT_in = sem("xT_in")
        xres_in = sem("xres_in")
        st_done, exp_done, mask_done = sem("st_done"), sem("exp_done"), sem("mask_done")
        s_done, max_done, msplit = sem("s_done"), sem("max_done"), sem("msplit")
        pv_done, o_evac, raw_out = sem("pv_done"), sem("o_evac"), sem("raw_out")
        sm_in, oc_in, rcp_done, rec_out = sem("sm_in"), sem("oc_in"), sem("rcp_done"), sem("rec_out")
        rb_in, on_done = sem("rb_in"), sem("on_done")
        mrow_out, mrow_in = sem("mrow_out"), sem("mrow_in")
        done = {k: sem(f"{k}_done") for k in MISC}
        evac = {k: sem(f"{k}_evac") for k in MISC}
        rope_done, p1_done, p2_done = sem("rope_done"), sem("p1_done"), sem("p2_done")
        r1_done, p3_done, qk_out = sem("r1_done"), sem("p3_done"), sem("qk_out")
        fill = [sem(f"fill{g}") for g in range(NG)]
        vcopy = sem("vcopy")
        st6 = [sem("ln1_stats"), sem("ln2_stats")]
        mv2 = [sem("ln1_mv"), sem("ln2_mv")]
        ve1 = [sem("ln1_ve"), sem("ln2_ve")]
        pw1 = [sem("ln1_pow"), sem("ln2_pow")]
        lnd = [sem("ln1_done"), sem("ln2_done")]
        x1b_done, gelu_done, out_sent = sem("x1b_done"), sem("gelu_done"), sem("out_sent")
        c_in, w_in, wx_in, c_ready = sem("c_in"), sem("w_in"), sem("wx_in"), sem("c_ready")
        lora_mm, lora_add = sem("lora_mm"), sem("lora_add")
        win_in = [sem("up_w_in"), sem("down_w_in")]
        bf = [sem("up_stage"), sem("down_stage")]
        bx = [sem("up_cross"), sem("down_cross")]
        su_mm, su_ev = sem("su_mm"), sem("su_ev")
        pool_c = sem("pool_c")

        passed = {nc.sync: sem("sp_passed"), nc.vector: sem("dve_passed"), nc.gpsimd: sem("pool_passed")}

        FILLN = 9 * DMA
        N_CONST = 11

        block = ctx.enter_context(nc.Block())

        def each(eng, one):
            for i in (-1, 0, 1):
                for s in steps(i, True):
                    one(s)
            with eng.Fori(2, B - 1) as i:
                for s in steps(i, False):
                    one(s)
            for i in (B - 1, B):
                for s in steps(i, True):
                    one(s)

        def wait(eng, s, value):
            if isinstance(value, int) and value <= 0:
                return
            eng.wait_ge(s, value)

        def hold(eng, s, value):
            if isinstance(value, int):
                wait(eng, s, value)
            else:
                eng.wait_ge(s, value)
                eng.sem_inc(passed[eng], 1)

        @block.sync
        def _(sp):
            sp.dma_start(ident[:, :], ident_d).then_inc(c_in, DMA)
            sp.dma_start(rot[:, 0, 0:2 * P], mask_d).then_inc(c_in, DMA)
            sp.dma_start(lora_a[:, 0, :], aqT_d).then_inc(c_in, DMA)
            sp.dma_start(lora_a[:, 1, :], avT_d).then_inc(c_in, DMA)
            sp.dma_start(lora_b[:, 0, :], bq_d).then_inc(c_in, DMA)
            sp.dma_start(lora_b[:, 1, :], bv_d).then_inc(c_in, DMA)
            sp.dma_start(w_x[:, 0, :, :, :], upx_d).then_inc(c_in, DMA)
            sp.dma_start(w_x[:, 1, :, :, :], dnx_d).then_inc(c_in, DMA)
            sp.dma_start(gbias[:, :], upbias_d).then_inc(c_in, DMA)
            sp.dma_start(bias_out[:, :], bcon_d.partition_broadcast(P)).then_inc(c_in, DMA)
            sp.dma_start(tmp_x[:, 0:D], dbias_d.partition_broadcast(P)).then_inc(c_in, DMA)
            for s in range(STAGES_IN):
                for k, d in enumerate((upin_d, dnin_d)):
                    if s:
                        sp.wait_ge(bf[k], 6 * s)
                    sp.dma_start(win[k], d[s, :].partition_broadcast(P)).then_inc(win_in[k], DMA)
                if s == 0:
                    sp.dma_start(tup[1], wexpT_d.rearrange("(b p) c -> p b c", p=P)).then_inc(wx_in, DMA)
                    sp.dma_start(tdn[0], wcon_d.rearrange("(b p) c -> p b c", p=P)).then_inc(wx_in, DMA)
                    sp.dma_start(wqk[:, :, :], wqk_d.rearrange("(k p) c -> p k c", p=P)).then_inc(w_in, DMA)
                    sp.dma_start(wv[:, :, :], wv_d.rearrange("(k p) c -> p k c", p=P)).then_inc(w_in, DMA)
                    sp.dma_start(wo[:, :, :], wo_d.rearrange("(k p) c -> p k c", p=P)).then_inc(w_in, DMA)
                    sp.dma_start(cosT[:, :], cos_d).then_inc(w_in, DMA)
                    sp.dma_start(sinT[:, :], sin_d).then_inc(w_in, DMA)
                    sp.dma_start(xT[:, :, :], xT_d[0, :, :].rearrange("(k p) t -> p k t", p=P))\
                      .then_inc(xT_in, DMA)

            def one(step):
                kind, b, n = step
                if kind == "XTL":
                    hold(sp, done["QK"], 4 * b)
                    hold(sp, done["V"], 2 * b)
                    sp.dma_start(xT[:, :, :], xT_d[b, :, :].rearrange("(k p) t -> p k t", p=P))\
                      .then_inc(xT_in, DMA)
                elif kind == "XRES":
                    hold(sp, evac["W2"], 2 * b)
                    sp.dma_start(x_res[:, :, :], x_d[b, :, :].rearrange("(a p) c -> p a c", p=P))\
                      .then_inc(xres_in, DMA)
                elif kind == "QKW":
                    hold(sp, p3_done, 2 * b + n + 1)
                    sp.dma_start(qk_scr[b, n, :, :, :].rearrange("(e i) h t -> (i h) e t", i=8),
                                 parts[:, n, :, :, :].rearrange("p a e t -> p (a e) t"))\
                      .then_inc(qk_out, DMA)
                elif kind == "FILL":
                    hold(sp, qk_out, 2 * DMA * (b + 1))
                    hold(sp, st_done, NU * (b - 1) + UG * (n + 1))
                    hs = slice(GH * n, GH * n + GH)
                    for first, rows in ((0, 3), (3, 2), (5, 1)):
                        sp.dma_start(q_st[DH * first:DH * (first + rows), hs, :],
                                     qk_scr[b, 0, 0:DH * rows, hs, :]).then_inc(fill[n], DMA)
                    for row, (_, part) in enumerate(PRODUCTS):
                        sp.dma_start(k_st[DH * row:DH * (row + 1), hs, :],
                                     qk_scr[b, 1, DH * part:DH * (part + 1), hs, :])\
                          .then_inc(fill[n], DMA)
                elif kind == "MROW":
                    hold(sp, evac["MT"], NG * b + n + 1)
                    sp.dma_start(m_scr[b, n, :, :], m_row[:, :]).then_inc(mrow_out, DMA)
                    hold(sp, mrow_out, DMA * (NG * b + n + 1))
                    sp.dma_start(q_st[NK:NK + NPART, GH * n:GH * n + GH, :],
                                 m_scr[b, n, :, :].rearrange("(a h) t -> a h t", a=NPART))\
                      .then_inc(mrow_in, DMA)
                elif kind == "RAW":
                    hold(sp, o_evac, NG * b + n + 1)
                    sp.dma_start(o_scr[b, n, :, :], o_raw[:, :]).then_inc(raw_out, DMA)
                elif kind == "SMOC":
                    hold(sp, raw_out, DMA * (NG * b + 2 * n + 2))
                    hold(sp, done["WO"], 2 * b)
                    hold(sp, rcp_done, 2 * b + n)
                    both = o_scr[b, 2 * n:2 * n + 2, :, :].rearrange("g (h r) t -> (g h) r t", h=GH)
                    sp.dma_start(s_m[:, :], both[:, DH, :].rearrange("h (c t) -> h c t", c=8))\
                      .then_inc(sm_in, DMA)
                    sp.dma_start(o_c[:, n, :], both[:, 0:DH, :]).then_inc(oc_in, DMA)
                elif kind == "REC":
                    hold(sp, rcp_done, 2 * b + n + 1)
                    sp.dma_start(r_scr[b, n, :, :].rearrange("h (c t) -> (h c) t", c=8), r_m[:, :])\
                      .then_inc(rec_out, DMA)
                    hold(sp, rec_out, DMA * (2 * b + n + 1))
                    hold(sp, on_done, 2 * b)
                    sp.dma_start(r_b[:, n, :],
                                 r_scr[b, n, :, :].unsqueeze(1).broadcast_to([8, DH, T]))\
                      .then_inc(rb_in, DMA)
                elif kind == "OUT":
                    hold(sp, lnd[1], b + 1)
                    sp.dma_start(out_d[b, :, :].rearrange("(a p) c -> p a c", p=P), y[:, :, :])\
                      .then_inc(out_sent, DMA)

            each(sp, one)
            sp.wait_ge(out_sent, DMA * B)

        @block.tensor
        def _(pe):
            pe.wait_ge(c_in, DMA * N_CONST)
            n = 0
            for w in range(2):
                for k in range(KD):
                    if n:
                        pe.wait_ge(lora_add, n)
                    pe.matmul(ps_m[:, 0:D], lora_a[:, w, k * P:(k + 1) * P], lora_b[:, w, :],
                              start=True, stop=True).then_inc(lora_mm, 1)
                    n += 1
            pe.wait_ge(lora_add, n)
            pe.wait_ge(bf[0], 6 * STAGES_IN + 1)
            pe.wait_ge(wx_in, 2 * DMA)
            m_up = mat[0][STAGES_IN % 2].rearrange("p (b c) -> p b c", b=NHT)
            m_dn = mat[1][STAGES_IN % 2].rearrange("p (b c) -> p b c", b=NHT)
            ev = 0
            for t in range(NHT):
                if ev:
                    pe.wait_ge(su_ev, ev)
                pe.matmul(ps_m[:, 0:D + 1], m_up[:, t, :], tup[1][:, t, :], start=True, stop=True)\
                  .then_inc(su_mm, 1)
                ev += 1
            pe.wait_ge(bf[1], 6 * STAGES_IN + 1)
            pe.wait_ge(bx[1], STAGES_X * 16)
            for t in range(NHT):
                pe.wait_ge(su_ev, ev)
                pe.matmul(ps_m[:, 0:D], m_dn[:, t, :], tdn[STAGES_X % 2][:, t, :],
                          start=True, stop=True).then_inc(su_mm, 1)
                ev += 1
            pe.wait_ge(bx[0], STAGES_X * 16)
            for k in range(KD):
                for half in range(2):
                    pe.wait_ge(su_ev, ev)
                    for t in range(4):
                        mm = pe.transpose(ps_m[:, t * P:(t + 1) * P],
                                          tup[STAGES_X % 2][:, 4 * half + t, k * P:(k + 1) * P],
                                          ident[:, :])
                    mm.then_inc(su_mm, 1)
                    ev += 1
            pe.wait_ge(su_ev, ev)
            last = [None]

            def one(step):
                kind, b, n = step
                if kind in MISC:
                    if last[0] is not None:
                        k0, b0, n0 = last[0]
                        wait(pe, evac[k0], PER[k0] * b0 + n0 + 1)
                    last[0] = step
                if kind == "QK":
                    pe.wait_ge(xT_in, DMA * (b + 1))
                    for k in range(KD):
                        mm = pe.matmul(ps_m[:, :], wqk[:, k, n * P:(n + 1) * P], xT[:, k, :],
                                       start=(k == 0), stop=(k == KD - 1))
                    mm.then_inc(done["QK"], 1)
                elif kind == "V":
                    for j in range(2):
                        for k in range(KD):
                            mm = pe.matmul(ps_m[:, j * D:(j + 1) * D],
                                           xT[:, k, (2 * n + j) * P:(2 * n + j + 1) * P], wv[:, k, :],
                                           start=(k == 0), stop=(k == KD - 1))
                    mm.then_inc(done["V"], 1)
                elif kind == "S":
                    g, u = n // UG, n % UG
                    if u == 0:
                        pe.wait_ge(fill[g], FILLN * (b + 1))
                    wait(pe, max_done, NU * b + n)

                    def s_mm(off, qt, k0, k1, start):
                        h = hd
                        return pe.matmul(ps_s[:, off:off + (k1 - k0)],
                                         q_st[0:NK, h, pos(qt) * P:(pos(qt) + 1) * P],
                                         k_st[0:NK, h, k0:k1], start=start, stop=False,
                                         skip_group_check=True)

                    def s_mask(o, cols):
                        m = maskb[:, 0:P] if cols == P else \
                            maskb[:, :].rearrange("p (a c) -> p a c", a=2)
                        return pe.matmul(o, identb[:, :], m, start=False, stop=True,
                                         skip_group_check=True)

                    def pairs(bank):
                        return ps_s[:, bank * T:(bank + 1) * T].rearrange("p (a c) -> p a c", a=2)
                    if u < GH:
                        hd = GH * g + u
                        s_mm(0, 3, 0, T, True)
                        s_mask(ps_s[:, 2 * P:3 * P], P)
                        s_mm(T, 2, 0, 2 * P, True)
                        s_mm(T + 2 * P, 2, 3 * P, T, False)
                        s_mm(T + 3 * P, 0, 3 * P, T, False)
                        mm = s_mask(pairs(1)[:, :, P:2 * P], 2 * P)
                    else:
                        for j in range(GH):
                            hd = GH * g + j
                            s_mm(2 * P * j, 1, 0, P, j % 2 == 0)
                            s_mm(2 * P * j + P, 1, 3 * P, T, False)
                            if j % 2:
                                mm = s_mask(pairs(j // 2)[:, :, 0:P], 2 * P)
                    mm.then_inc(s_done, 1)
                elif kind == "ST":
                    g, u = n // UG, n % UG
                    if u == 0:
                        pe.wait_ge(mrow_in, DMA * (NG * b + g + 1))
                    wait(pe, exp_done, NU * b + n - 1)
                    dst = ps_t[:, n % 2, :]

                    def t_mm(off, h, kt, q0, q1, start):
                        return pe.matmul(dst[:, off:off + (q1 - q0)],
                                         k_st[0:NK + NPART, h, pos(kt) * P:(pos(kt) + 1) * P],
                                         q_st[0:NK + NPART, h, q0:q1], start=start, stop=True,
                                         skip_group_check=True)
                    if u < GH:
                        h = GH * g + u
                        t_mm(0, h, 0, 0, T, True)
                        t_mm(T, h, 3, 2 * P, 3 * P, True)
                        mm = t_mm(T + P, h, 1, 0, 3 * P, False)
                    else:
                        for j in range(GH):
                            mm = t_mm(2 * P * j, GH * g + j, 2, P, 3 * P, j % 2 == 0)
                    mm.then_inc(st_done, 1)
                elif kind == "MT":
                    pe.wait_ge(msplit, NPART * (NG * b + n + 1) + NG * b + n + 1)
                    for t in range(NT):
                        mm = pe.transpose(ps_mb[0:NPART * GH, t * P:(t + 1) * P],
                                          m_part[:, t, :, :].rearrange("p a h -> p (a h)"),
                                          identb[:, :])
                    mm.then_inc(done["MT"], 1)
                elif kind == "PV":
                    g, c = n // 4, n % 4
                    if c == 0:
                        pe.wait_ge(vcopy, b + 1)
                        wait(pe, o_evac, NG * b + g)
                        pe.wait_ge(mask_done, NU * b + UG * g + GH)
                    if c == 3:
                        pe.wait_ge(mask_done, NU * b + UG * g + UG)
                    kt, q0, q1, off = [(0, 0, T, 0), (1, 0, 3 * P, T + P), (3, 2 * P, 3 * P, T),
                                       (2, P, 3 * P, None)][c]
                    for j in range(GH):
                        src = pT[:, g % 2, j, off:off + q1 - q0] if off is not None else \
                            pT[:, g % 2, GH, 2 * P * j:2 * P * (j + 1)]
                        mm = pe.matmul(ps_o[32 * j:32 * j + 32, q0:q1],
                                       v_aug[:, pos(kt), GH * g + j, :], src,
                                       start=(c == 0), stop=(c == 3), skip_group_check=True)
                    if c == 3:
                        mm.then_inc(pv_done, 1)
                elif kind == "WO":
                    pe.wait_ge(on_done, 2 * b + 2)
                    for j in range(2):
                        t = 2 * n + j
                        for k in range(KD):
                            mm = pe.matmul(ps_m[:, j * D:(j + 1) * D], o_c[:, k, t * P:(t + 1) * P],
                                           wo[:, k, :], start=(k == 0), stop=(k == KD - 1))
                    mm.then_inc(done["WO"], 1)
                elif kind == "XT":
                    pe.wait_ge(lnd[0], b + 1)
                    for t in range(NT):
                        mm = pe.transpose(ps_m[:, t * P:(t + 1) * P], x1[:, t, n * P:(n + 1) * P],
                                          ident[:, :])
                    mm.then_inc(done["XT"], 1)
                elif kind == "W1":
                    if n == 0:
                        pe.wait_ge(evac["XT"], 2 * b + 2)
                    for k in range(KD):
                        mm = pe.matmul(ps_m[:, :], w1[:, k, n * P:(n + 1) * P], x1T[:, k, :],
                                       start=(k == 0), stop=(k == KD - 1))
                    mm.then_inc(done["W1"], 1)
                elif kind == "W2":
                    pe.wait_ge(gelu_done, 2 * b + 2)
                    for j in range(2):
                        t = 2 * n + j
                        for k in range(NHT):
                            mm = pe.matmul(ps_m[:, j * D:(j + 1) * D], gact[:, k, t * P:(t + 1) * P],
                                           w2[:, k, :], start=(k == 0), stop=(k == NHT - 1))
                    mm.then_inc(done["W2"], 1)

            for i in (-1, 0, 1):
                for s in steps(i, True):
                    one(s)
            with pe.Fori(2, B - 1) as i:
                last[0] = ("W2", i - 2, 1)
                for s in steps(i, False):
                    one(s)
            last[0] = ("W2", B - 3, 1)
            for i in (B - 1, B):
                for s in steps(i, True):
                    one(s)

        @block.scalar
        def _(act):
            def one(step):
                kind, b, n = step
                if kind == "ST":
                    g, u = n // UG, n % UG
                    act.wait_ge(st_done, NU * b + n + 1)
                    if u == 0:
                        wait(act, pv_done, NG * b + g - 1)
                    act.activation(pT[:, g % 2, u, :], ps_t[:, n % 2, :], ACT.Exp, scale=SCALE)\
                       .then_inc(exp_done, 1)
                elif kind == "OE":
                    act.wait_ge(pv_done, NG * b + n + 1)
                    wait(act, raw_out, DMA * (NG * b + n))
                    act.activation(o_raw[:, :], ps_o[:, :], ACT.Copy).then_inc(o_evac, 1)
                elif kind == "V":
                    act.wait_ge(done["V"], 2 * b + n + 1)
                    wait(act, vcopy, b)
                    act.activation(v_new[:, 2 * n:2 * n + 2, :].rearrange("p a c -> p (a c)"),
                                   ps_m[:, :], ACT.Copy).then_inc(evac["V"], 1)
                elif kind == "VC":
                    wait(act, pv_done, NG * b)
                    act.wait_ge(evac["V"], 2 * b + 2)
                    act.wait_ge(pool_c, 1)
                    act.activation(v_aug[:, :, :, 0:DH],
                                   v_new[:, :, :].rearrange("p a (h d) -> p a h d", h=H), ACT.Copy)\
                       .then_inc(vcopy, 1)
                elif kind == "SPLIT":
                    act.wait_ge(rope_done, 2 * b + n + 1)
                    wait(act, qk_out, DMA * (2 * b - 1 + n))
                    act.activation(parts[:, n, 0, :, :], rot[:, :, :], ACT.Copy).then_inc(p1_done, 1)
                    act.wait_ge(r1_done, 2 * b + n + 1)
                    act.activation(parts[:, n, 1, :, :], rot[:, :, :], ACT.Copy).then_inc(p2_done, 1)
                elif kind == "XT":
                    act.wait_ge(done["XT"], 2 * b + n + 1)
                    wait(act, done["W1"], NHT * b)
                    act.activation(x1T[:, n, :], ps_m[:, :], ACT.Copy).then_inc(evac["XT"], 1)
                elif kind == "GE":
                    act.wait_ge(evac["W1"], NHT * b + 4 * (n + 1))
                    half = gact[:, 4 * n:4 * n + 4, :]
                    act.activation(half, half, ACT.Gelu).then_inc(gelu_done, 1)

            each(act, one)

        @block.vector
        def _(dve):
            dve.wait_ge(c_in, DMA * N_CONST)
            dve.tensor_copy(identb[:, :], ident[:, :]).then_inc(c_ready, 1)
            dve.tensor_copy(maskb[:, :], rot[:, 0, 0:2 * P]).then_inc(c_ready, 1)
            dve.tensor_tensor(bias_out[:, :], bias_out[:, :], tmp_x[:, 0:D], ALU.add)\
               .then_inc(c_ready, 1)
            dve.wait_ge(w_in, 5 * DMA)
            n = 0
            for dst, off in ((wqk, 0), (wv, 0)):
                for k in range(KD):
                    dve.wait_ge(lora_mm, n + 1)
                    dve.scalar_tensor_tensor(out=dst[:, k, 0:D], in0=ps_m[:, 0:D], scalar=LORA,
                                             in1=dst[:, k, 0:D], op0=ALU.mult, op1=ALU.add)\
                       .then_inc(lora_add, 1)
                    n += 1
            butterfly_in(dve, 0, ident, mat[0], win[0], win_in[0], bf[0], tmp_v, ident_ready=None)
            for t in range(NHT):
                dve.wait_ge(su_mm, t + 1)
                dve.tensor_copy(tup[0][:, t, :], ps_m[:, 0:D + 1]).then_inc(su_ev, 1)
                if t == 0:
                    pass
            cross(dve, tdn, w_x[:, 1, :, :, :], bx[1], tmp_x[:, 0:D], D, order=(2, 1, 0))
            cross(dve, tup, w_x[:, 0, :, :, :], bx[0], tmp_v[:, 0:D + 1], D + 1, order=(0, 1, 2),
                  ready=(su_ev, NHT))
            for t in range(NHT):
                dve.wait_ge(su_mm, NHT + t + 1)
                dve.tensor_copy(w2[:, t, :], ps_m[:, 0:D]).then_inc(su_ev, 1)
            for k in range(KD):
                for half in range(2):
                    dve.wait_ge(su_mm, 2 * NHT + 2 * k + half + 1)
                    dve.tensor_copy(w1[:, k, T * half:T * (half + 1)], ps_m[:, :]).then_inc(su_ev, 1)
            dve.tensor_tensor(gbias[:, :], gbias[:, :], tup[STAGES_X % 2][:, :, D], ALU.add)\
               .then_inc(c_ready, 1)
            dve.wait_ge(su_ev, 2 * NHT + 4)
            dve.wait_ge(c_ready, 4)
            dve.memset(k_st[96:P, :, :], 1.0).then_inc(c_ready, 1)
            dve.wait_ge(c_ready, 5)

            def one(step):
                kind, b, n = step
                if kind == "S":
                    g, u = n // UG, n % UG
                    dve.wait_ge(s_done, NU * b + n + 1)
                    if u < GH:
                        for off, cols, qt in ((0, T, 3), (T, 3 * P, 2), (T + 3 * P, P, 0)):
                            ins = dve.tensor_reduce(m_raw[:, pos(qt), u:u + 1], ps_s[:, off:off + cols],
                                                    AX.X, ALU.max, negate=True)
                        ins.then_inc(max_done, 1)
                    else:
                        dve.tensor_reduce(m_raw[:, pos(1), :],
                                          ps_s[:, :].rearrange("p (h c) -> p h c", h=GH),
                                          AX.X, ALU.max, negate=True).then_inc(max_done, 1)
                        c0 = 4 * (NG * b + g)
                        dve.wait_ge(max_done, NU * b + n + 1)
                        wait(dve, done["MT"], NG * b + g)
                        dve.tensor_copy(m_part[:, :, 0, :], m_raw[:, :, :]).then_inc(msplit, 1)
                        dve.wait_ge(msplit, c0 + 1)
                        dve.tensor_tensor(m_res[:, :, :], m_raw[:, :, :], m_part[:, :, 0, :],
                                          ALU.subtract).then_inc(msplit, 1)
                        dve.wait_ge(msplit, c0 + 2)
                        dve.tensor_copy(m_part[:, :, 1, :], m_res[:, :, :]).then_inc(msplit, 1)
                        dve.wait_ge(msplit, c0 + 3)
                        dve.tensor_tensor(m_part[:, :, 2, :], m_res[:, :, :], m_part[:, :, 1, :],
                                          ALU.subtract).then_inc(msplit, 1)
                elif kind == "MT":
                    dve.wait_ge(done["MT"], NG * b + n + 1)
                    wait(dve, mrow_out, DMA * (NG * b + n))
                    dve.tensor_copy(m_row[:, :], ps_mb[0:NPART * GH, 0:T]).then_inc(evac["MT"], 1)
                elif kind == "QK":
                    dve.wait_ge(done["QK"], 4 * b + n + 1)
                    if n % 2 == 0:
                        wait(dve, rope_done, 2 * b + n // 2)
                    a, c = ((0, cosT), (1, sinT)) if n % 2 == 0 else ((2, sinT), (3, cosT))
                    dve.tensor_tensor(rope_in[:, a[0], :], ps_m[:, :], a[1][:, :], ALU.mult)
                    dve.tensor_tensor(rope_in[:, c[0], :], ps_m[:, :], c[1][:, :], ALU.mult)\
                       .then_inc(evac["QK"], 1)
                elif kind == "SPLIT":
                    dve.wait_ge(p1_done, 2 * b + n + 1)
                    dve.tensor_tensor(rot[:, :, :], rot[:, :, :], parts[:, n, 0, :, :], ALU.subtract)\
                       .then_inc(r1_done, 1)
                    dve.wait_ge(p2_done, 2 * b + n + 1)
                    dve.tensor_tensor(parts[:, n, 2, :, :], rot[:, :, :], parts[:, n, 1, :, :],
                                      ALU.subtract).then_inc(p3_done, 1)
                elif kind == "RCP":
                    dve.wait_ge(sm_in, DMA * (2 * b + n + 1))
                    wait(dve, rec_out, DMA * (2 * b + n))
                    dve.reciprocal(r_m[:, :], s_m[:, :]).then_inc(rcp_done, 1)
                elif kind == "WO":
                    dve.wait_ge(done["WO"], 2 * b + n + 1)
                    if n == 0:
                        dve.wait_ge(xres_in, DMA * (b + 1))
                        wait(dve, x1b_done, b)
                        wait(dve, done["XT"], 2 * b)
                    dve.tensor_tensor(x1[:, 2 * n:2 * n + 2, :].rearrange("p a c -> p (a c)"),
                                      ps_m[:, :],
                                      x_res[:, 2 * n:2 * n + 2, :].rearrange("p a c -> p (a c)"),
                                      ALU.add).then_inc(evac["WO"], 1)
                elif kind == "W1":
                    dve.wait_ge(done["W1"], NHT * b + n + 1)
                    if n == 0:
                        wait(dve, done["W2"], 2 * b)
                    dve.tensor_scalar(gact[:, n, :], ps_m[:, :], gbias[:, n:n + 1], None, ALU.add)\
                       .then_inc(evac["W1"], 1)
                elif kind == "W2":
                    dve.wait_ge(done["W2"], 2 * b + n + 1)
                    if n == 0:
                        dve.wait_ge(x1b_done, b + 1)
                        wait(dve, out_sent, DMA * b)
                    dve.tensor_tensor(y[:, 2 * n:2 * n + 2, :].rearrange("p a c -> p (a c)"),
                                      ps_m[:, :],
                                      x_res[:, 2 * n:2 * n + 2, :].rearrange("p a c -> p (a c)"),
                                      ALU.add).then_inc(evac["W2"], 1)
                elif kind == "LNA":
                    src = (x1, y)[n]
                    dve.wait_ge((evac["WO"], evac["W2"])[n], 2 * b + 2)
                    for t in range(NT):
                        ins = dve.bn_stats(stats[:, n, t, :], src[:, t, :])
                    ins.then_inc(st6[n], 1)
                    hold(dve, st6[n], b + 1)
                    for t in range(NT):
                        ins = dve.bn_aggr(mv[:, n, t, :], stats[:, n, t, :])
                    ins.then_inc(mv2[n], 1)
                    dve.wait_ge(mv2[n], b + 1)
                    dve.tensor_scalar(ve[:, n, :], mv[:, n, :, 1], EPS, None, ALU.add)\
                       .then_inc(ve1[n], 1)
                elif kind == "LNB":
                    src = (x1, y)[n]
                    dve.wait_ge(pw1[n], b + 1)
                    for t in range(NT):
                        ins = dve.tensor_scalar(src[:, t, :], src[:, t, :], mv[:, n, t, 0:1],
                                                rstd[:, n, t:t + 1], ALU.subtract, ALU.mult)
                    ins.then_inc(lnd[n], 1)

            each(dve, one)

        @block.gpsimd
        def _(pool):
            pool.memset(mhalf[:, :], -0.5)
            pool.memset(v_aug[:, :, :, :], 1.0).then_inc(pool_c, 1)
            pool.wait_ge(c_in, DMA * N_CONST)
            butterfly_in(pool, 1, ident, mat[1], win[1], win_in[1], bf[1], tmp_p, ident_ready=None)

            def one(step):
                kind, b, n = step
                if kind == "ST":
                    g, u = n // UG, n % UG
                    hold(pool, exp_done, NU * b + n + 1)
                    if u < GH:
                        v = pT[:, g % 2, u, 3 * P:6 * P].rearrange("p (a c) -> p a c", a=3)
                    else:
                        v = pT[:, g % 2, u, :].rearrange("p (a c) -> p a c", a=GH)[:, :, 0:P]
                    pool.affine_select(out=v, in_=v, compare_op=ALU.is_ge, fill=0.0, base=0,
                                       pattern=[[0, 3 if u < GH else GH], [1, P]],
                                       channel_multiplier=-1).then_inc(mask_done, 1)
                elif kind == "ROPE":
                    pool.wait_ge(evac["QK"], 4 * b + 2 * n + 2)
                    wait(pool, p3_done, 2 * b + n)
                    pool.tensor_tensor(rot[:, 0, :], rope_in[:, 0, :], rope_in[:, 2, :], ALU.subtract)
                    pool.tensor_tensor(rot[:, 1, :], rope_in[:, 1, :], rope_in[:, 3, :], ALU.add)\
                        .then_inc(rope_done, 1)
                elif kind == "ON":
                    pool.wait_ge(rb_in, DMA * (2 * b + n + 1))
                    pool.wait_ge(oc_in, DMA * (2 * b + n + 1))
                    pool.tensor_tensor(o_c[:, n, :], o_c[:, n, :], r_b[:, n, :], ALU.mult)\
                        .then_inc(on_done, 1)
                elif kind == "LNA":
                    pool.wait_ge(ve1[n], b + 1)
                    pool.tensor_tensor(rstd[:, n, :], ve[:, n, :], mhalf[:, :], ALU.pow)\
                        .then_inc(pw1[n], 1)
                elif kind == "LNB" and n == 0:
                    pool.wait_ge(lnd[0], b + 1)
                    pool.wait_ge(c_ready, 3)
                    pool.tensor_tensor(x_res[:, :, :], x1[:, :, :],
                                       bias_out[:, :].unsqueeze(1).broadcast_to([P, NT, D]), ALU.add)\
                        .then_inc(x1b_done, 1)

            each(pool, one)


def butterfly_in(eng, which, ident, mat, w, w_in, stage, tmp, ident_ready):
    a0 = mat[0].rearrange("p (b c) -> p b c", b=NHT)
    eng.tensor_copy(a0, ident[:, :].unsqueeze(1).broadcast_to([P, NHT, P])).then_inc(stage, 1)
    n = 1
    eng.wait_ge(stage, n)
    wv = w.rearrange("p (x k) -> p x k", x=4)
    t = tmp.rearrange("p (x k) -> p x k", x=2)
    for s in range(STAGES_IN):
        size = 2 ** s if which == 0 else 2 ** (STAGES_IN - 1 - s)
        src = mat[s % 2].rearrange("p (n x k) -> p n x k", x=2, k=size)
        dst = mat[(s + 1) % 2].rearrange("p (n x k) -> p n x k", x=2, k=size)
        eng.wait_ge(w_in, DMA * (s + 1))
        for half in range(2):
            for x in range(2):
                eng.tensor_tensor(t[:, x, :].rearrange("p (n k) -> p n k", k=size), src[:, :, x, :],
                                  wv[:, 2 * half + x, :].rearrange("p (n k) -> p n k", k=size),
                                  ALU.mult).then_inc(stage, 1)
                n += 1
            eng.wait_ge(stage, n)
            last = eng.tensor_tensor(dst[:, :, half, :], t[:, 0, :].rearrange("p (n k) -> p n k", k=size),
                                     t[:, 1, :].rearrange("p (n k) -> p n k", k=size), ALU.add)
            last.then_inc(stage, 1)
            n += 1
            eng.wait_ge(stage, n)


def cross(eng, bufs, w, count, tmp, cols, order, ready=None):
    n = 0
    if ready:
        eng.wait_ge(*ready)
    for i, st in enumerate(order):
        src, dst = bufs[i % 2], bufs[(i + 1) % 2]
        size = 2 ** st
        for p in range(4):
            a = (p // size) * 2 * size + p % size
            for half in range(2):
                first, second = w[:, st, 2 * half, p:p + 1], w[:, st, 2 * half + 1, p:p + 1]
                eng.tensor_scalar(tmp, src[:, a + size, :], second, None, ALU.mult).then_inc(count, 1)
                n += 1
                eng.wait_ge(count, n)
                eng.scalar_tensor_tensor(out=dst[:, a + size * half, :], in0=src[:, a, :],
                                         scalar=first, in1=tmp, op0=ALU.mult, op1=ALU.add)\
                   .then_inc(count, 1)
                n += 1
                eng.wait_ge(count, n)


def kernel(**inputs):
    import numpy as np
    import concourse.bacc as bacc
    from concourse.bass_utils import run_bass_kernel_spmd as run

    def inp(name):
        return np.asarray(inputs["L0_" + name])

    x = inp("attn_query")
    order = np.concatenate([np.arange(P, T), np.arange(P)])
    xp = x[:, order, :]
    xT = np.zeros((B + 1, D, T), x.dtype)
    xT[:B] = xp.transpose(0, 2, 1)
    pair, head = np.meshgrid(np.arange(DH // 2), np.arange(H), indexing="ij")
    even = (head * DH + 2 * pair).ravel()
    eo = np.concatenate([even, even + 1])
    wqk = np.concatenate([inp("attn_wq")[:, eo], inp("attn_wk")[:, eo]], axis=1)

    def stage_weights(w, turned):
        w = w.reshape(w.shape[0], NPAIR, 4).transpose(0, 2, 1)
        return w[:, [0, 2, 1, 3]] if turned else w

    up, down = stage_weights(inp("ffn_up_weights"), False), stage_weights(inp("ffn_down_weights"), True)

    def across(w):
        return w[STAGES_IN:].reshape(STAGES_X, 4, 4, P).transpose(3, 0, 1, 2)

    i = np.arange(0, DH, 2, dtype=np.float32) / DH
    theta = order.astype(np.float32)[:, None] / np.float32(10000.0) ** i[None, :]
    theta = np.repeat(theta.T.astype(np.float64), H, axis=0)
    tri = np.where(np.arange(P)[None, :] > np.arange(P)[:, None], np.float32(-1e30), np.float32(0))

    arrays = {
        "xT": xT,
        "x": xp,
        "wqk": wqk,
        "wv": inp("attn_wv"),
        "aqT": inp("attn_Aq").T,
        "bq": inp("attn_Bq")[:, eo],
        "avT": inp("attn_Av").T,
        "bv": inp("attn_Bv"),
        "wo": inp("attn_wo"),
        "wexpT": np.concatenate([inp("ffn_W_exp"), inp("ffn_b_exp")[None, :]], axis=0).T,
        "bexp": inp("ffn_b_exp"),
        "upin": up[:STAGES_IN].reshape(STAGES_IN, 4 * NPAIR),
        "upx": across(up),
        "upbias": inp("ffn_up_bias").reshape(NHT, P).T,
        "dnin": down[STAGES_IN - 1::-1].reshape(STAGES_IN, 4 * NPAIR),
        "dnx": across(down),
        "wcon": inp("ffn_W_con"),
        "bcon": inp("ffn_b_con"),
        "dbias": inp("ffn_down_bias"),
        "cos": np.cos(theta).astype(np.float32),
        "sin": np.sin(theta).astype(np.float32),
        "ident": np.eye(P, dtype=np.float32),
        "mask": np.concatenate([tri, tri], axis=1),
    }
    nc = bacc.Bacc("TRN2", target_bir_lowering=False, num_devices=1)
    args = []
    for name in arrays:
        arrays[name] = np.ascontiguousarray(arrays[name])
        a = arrays[name]
        args.append(nc.dram_tensor(f"in_{name}", a.shape, mybir.dt.from_np(a.dtype), kind="ExternalInput").ap())
    args.append(nc.dram_tensor("out_0", (B, T, D), FP32, kind="ExternalOutput").ap())
    layer(nc, *args)
    r = run(nc, [{f"in_{k}": v for k, v in arrays.items()}], core_ids=[0])
    got = r.results[0]["out_0"]
    return got[:, np.argsort(order), :]
```

```python
import concourse.bass as bass
from concourse import mybir
from contextlib import ExitStack

FP32 = mybir.dt.float32
BF16 = mybir.dt.bfloat16
ALU = mybir.AluOpType
ACT = mybir.ActivationFunctionType
AX = mybir.AxisListType

B, T, D = 16, 512, 256
H, DH = 16, 16
HID = 1024
P = 128
NT = T // P
KD = D // P
NHT = HID // P
GH = 4
NG = H // GH
UG = 5
NU = NG * UG
LEAD = 8
R = 8
NPART = 3
PRODUCTS = [(0, 0), (1, 0), (2, 0), (0, 1), (1, 1), (0, 2)]
NK = len(PRODUCTS) * DH
EPS = 1e-5
LORA = 4.0
SCALE = 0.25
STAGES_IN = 7
STAGES_X = 3
NPAIR = HID // 2
DMA = 16


def pos(tile):
    return (tile + NT - 1) % NT


def spread(when, kind, first, per):
    return [(when, first + k, kind, sum(per[:k]), c) for k, c in enumerate(per)]


SETUP_UNITS = (
    [(-1, 1, "BU", 0, 2), (-1, 6, "BU", 2, 3), (-1, 7, "BU", 5, 3)] +
    [(0, t, "BU", 8 + t, 1) for t in range(6)] +
    [(-1, 2, "BD", 0, 2), (-1, 6, "BD", 2, 2), (-1, 7, "BD", 4, 1)] +
    [(0, t, "BD", 5 + t, 1) for t in range(9)] +
    spread(0, "UM", 6, [1] * NHT) + [(0, 14, "ZL", 0, 1)] +
    spread(0, "XU", 14, [2] * 6) + [(1, 0, "XB", 0, 1)] + spread(1, "UT", 1, [1] * 4) +
    spread(1, "XD", 0, [1] * 12) + spread(1, "DM", 12, [2] * 4))


def steps(i, static):
    out = []

    def put(kind, b, n=0, top=B):
        if not static or 0 <= b < top:
            out.append((kind, b, n))

    def setup(when, kind, n=0):
        if static and i == when:
            out.append((kind, 0, n))

    first = {0: ("QK", i + 1, 0), 1: ("QK", i + 1, 1), 2: ("QK", i + 1, 2), 3: ("QK", i + 1, 3),
             4: ("W2", i - 2, 0), 5: ("W2", i - 2, 1), 6: ("W2", i - 2, 2), 7: ("W2", i - 2, 3),
             10: ("V", i + 1, 0), 11: ("WO", i - 1, 0), 12: ("WO", i - 1, 1),
             15: ("XT", i - 1, 0), 16: ("W1", i - 1, 0), 17: ("W1", i - 1, 2),
             14: ("V", i + 1, 1), 18: ("W1", i - 1, 4), 19: ("W1", i - 1, 6)}
    third = {3: ("MT", i, 1), 8: ("MT", i, 2), 13: ("MT", i, 3), 18: ("MT", i + 1, 0)}
    second = {15: ("XT", i - 1, 1), 16: ("W1", i - 1, 1),
             17: ("W1", i - 1, 3), 18: ("W1", i - 1, 5), 19: ("W1", i - 1, 7)}
    for t in range(NU):
        g, u = t // UG, t % UG
        if t == 0:
            put("OE", i - 1, 2)
            put("RAW", i - 1, 2)
        if t == 5:
            put("OE", i - 1, 3)
            put("VC", i)
            put("RAW", i - 1, 3)
        if t == 10:
            put("OE", i, 0)
            put("RAW", i, 0)
        if t == 15:
            put("OE", i, 1)
            put("RAW", i, 1)
        if t == 14:
            put("LNB", i - 1, 0)
        put("ST", i, t)
        if t in first:
            put(*first[t])
        if t + LEAD < NU:
            put("S", i, t + LEAD)
        else:
            put("S", i + 1, t + LEAD - NU)
        if t in second:
            put(*second[t])
        if u >= 1:
            if g == 0:
                put("PV", i - 1, 4 * (NG - 1) + u - 1)
            else:
                put("PV", i, 4 * (g - 1) + u - 1)
        if t in third:
            put(*third[t])
            put("MROW", third[t][1], third[t][2])
            put("FILL", *[(i, 3), (i + 1, 0), (i + 1, 1), (i + 1, 2)][g])
        if t == 0:
            put("ON", i - 1, 0)
            put("GE", i - 2)
        for n in range(2):
            if t == 3 * n + 1:
                put("ROPE", i + 1, n)
                put("PART0", i + 1, n)
            if t == 3 * n + 2:
                put("RES1", i + 1, n)
                put("PART1", i + 1, n)
            if t == 3 * n + 3:
                put("PART2", i + 1, n)
                put("QKW", i + 1, n)
        if t == 6:
            put("SMOC", i - 1, 1)
        if t == 7:
            put("RCP", i - 1, 1)
            put("REC", i - 1, 1)
            put("LNA", i - 2, 1)
        if t == 9:
            put("RB", i - 1, 1)
            put("ON", i - 1, 1)
            put("LNB", i - 2, 1)
            put("OUT", i - 2)
        if t == 12:
            put("LNA", i - 1, 0)
        if t == 13:
            put("XTL", i + 2, 0, B + 1)
            put("XRES", i)
        if t == 16:
            put("SMOC", i, 0)
        if t == 17:
            put("RCP", i, 0)
            put("REC", i, 0)
        if t == 19:
            put("RB", i, 0)
        for when, at, kind, n, count in SETUP_UNITS:
            if t == at:
                for k in range(n, n + count):
                    setup(when, kind, k)
    return out


PER = {"QK": 4, "V": 2, "MT": NG, "WO": 2, "XT": KD, "W1": NHT, "W2": NT, "UM": NHT, "UT": 4, "DM": NHT}


def layer(nc, xT_d, x_d, wqk_d, wv_d, lora_d, wo_d, wexpT_d, upin_d, dnin_d, wx_d, bx_d, wcon_d,
          bout_d, cs_d, ident_d, mask_d, out_d):
    ctx = ExitStack()
    with ctx:
        def sb(name, shape, dt=FP32):
            return ctx.enter_context(nc.sbuf_tensor(name, shape, dt))

        def pb(name, shape, dt=FP32):
            return ctx.enter_context(nc.psum_tensor(name, shape, dt))

        def sem(name):
            return ctx.enter_context(nc.semaphore(name))

        q_st = sb("q_st", [P, H, T], BF16)
        k_st = sb("k_st", [P, H, T], BF16)
        pT = sb("pT", [P, 2, UG, 2 * T])
        xT = sb("xT", [P, KD, T])
        cs = sb("cs", [P, 2, T])
        rope_in = sb("rope_in", [P, 2, 4, T])
        rot = sb("rot", [P, 2, T])
        parts = sb("parts", [P, 2, NPART, 2, T], BF16)
        v_new = sb("v_new", [P, NT, D])
        v_aug = sb("v_aug", [P, NT, H, 2 * DH])
        o_raw = sb("o_raw", [P, T])
        o_c = sb("o_c", [P, 2, T])
        r_b = sb("r_b", [P, 2, T])
        s_m = sb("s_m", [64, 64])
        r_m = sb("r_m", [64, 64])
        x_res = sb("x_res", [P, NT, D])
        x1 = sb("x1", [P, NT, D])
        x1b = sb("x1b", [P, NT, D])
        x1T = sb("x1T", [P, KD, T])
        gact = sb("gact", [P, NHT, T])
        y = sb("y", [P, NT, D])
        m_raw = sb("m_raw", [P, NT, GH])
        m_res = sb("m_res", [P, NT, GH])
        m_part = sb("m_part", [P, NT, NPART, GH], BF16)
        m_row = sb("m_row", [NPART * GH, T], BF16)
        wqk = sb("wqk", [P, KD, 4 * P])
        wv = sb("wv", [P, KD, D])
        wo = sb("wo", [P, KD, D])
        w1 = sb("w1", [P, KD, HID])
        w2 = sb("w2", [P, NHT, D])
        bias_out = sb("bias_out", [P, D])
        gbias = sb("gbias", [P, NHT])
        ident = sb("ident", [P, P])
        identb = sb("identb", [P, P], BF16)
        maskb = sb("maskb", [P, 2 * P], BF16)
        stats = sb("stats", [P, 2, NT, 6])
        mv = sb("mv", [P, 2, NT, 2])
        ve = sb("ve", [P, 2, NT])
        rstd = sb("rstd", [P, 2, NT])
        mhalf = sb("mhalf", [P, NT])
        lora = sb("lora", [R, 4, D])
        w_x = sb("w_x", [P, 2, STAGES_X, 4, 4])
        b_x = sb("b_x", [P, 2, NHT])
        b_t = sb("b_t", [P, 2, 4])
        b_u = sb("b_u", [P, 2, 4])
        mask = sb("mask", [P, 2 * P])
        tmp_x = sb("tmp_x", [P, 2, D])
        ga = gact[:, :, :].rearrange("p a c -> p (a c)")
        mat = [[ga[:, (2 * k + j) * HID:(2 * k + j + 1) * HID] for j in range(2)]
               for k in range(2)]
        win = [w1[:, :, :].rearrange("p a c -> p (a c)"), w2[:, :, :].rearrange("p a c -> p (a c)")]
        tmp_v = x1[:, :, :].rearrange("p a c -> p (a c)")
        tmp_p = x1T[:, :, :].rearrange("p a c -> p (a c)")
        half_up = (y, x1b)
        tile_up = [half_up[t // 4][:, t % 4, :] for t in range(NHT)]
        tile_dn = [ga[:, t * D:(t + 1) * D] for t in range(NHT)]

        ps_t = pb("ps_t", [P, 2, 2 * T])
        ps_s = pb("ps_s", [P, 2 * T])
        ps_o = pb("ps_o", [P, T])
        ps_m = pb("ps_m", [P, T])
        ps_mb = ps_m[:, :].bitcast(BF16)

        qk_scr = nc.dram_tensor("qk_scr", (B, 2, NPART * DH, H, T), BF16, kind="Internal").ap()
        o_scr = nc.dram_tensor("o_scr", (B, NG, P, T), FP32, kind="Internal").ap()
        m_scr = nc.dram_tensor("m_scr", (B, NG, NPART * GH, T), BF16, kind="Internal").ap()
        r_scr = nc.dram_tensor("r_scr", (B, 2, 8, T), FP32, kind="Internal").ap()

        xT_in = sem("xT_in")
        xres_in = sem("xres_in")
        st_done, exp_done, mask_done = sem("st_done"), sem("exp_done"), sem("mask_done")
        s_done, max_done, msplit = sem("s_done"), sem("max_done"), sem("msplit")
        pv_done, o_evac, raw_out = sem("pv_done"), sem("o_evac"), sem("raw_out")
        sm_in, oc_in, rcp_done, rec_out = sem("sm_in"), sem("oc_in"), sem("rcp_done"), sem("rec_out")
        rb_in, on_done = sem("rb_in"), sem("on_done")
        mrow_out, mrow_in = sem("mrow_out"), sem("mrow_in")
        done = {k: sem(f"{k}_done") for k in PER}
        evac = {k: sem(f"{k}_evac") for k in PER}
        rope_done, p1_done, p2_done = sem("rope_done"), sem("p1_done"), sem("p2_done")
        r1_done, p3_done, qk_out = sem("r1_done"), sem("p3_done"), sem("qk_out")
        fill = [sem(f"fill{g}") for g in range(NG)]
        vcopy = sem("vcopy")
        st6 = [sem("ln1_stats"), sem("ln2_stats")]
        mv2 = [sem("ln1_mv"), sem("ln2_mv")]
        ve1 = [sem("ln1_ve"), sem("ln2_ve")]
        pw1 = [sem("ln1_pow"), sem("ln2_pow")]
        lnd = [sem("ln1_done"), sem("ln2_done")]
        x1b_done, gelu_done, out_sent = sem("x1b_done"), sem("gelu_done"), sem("out_sent")
        c_in, w_in, wx_in, c_ready = sem("c_in"), sem("w_in"), sem("wx_in"), sem("c_ready")
        lo_in, cs_in, wz_in = sem("lora_in"), sem("cos_in"), sem("w_con_in")
        lora_mm, lora_add = sem("lora_mm"), sem("lora_add")
        win_in = [[sem(f"{w}_w{half}_in") for half in range(2)] for w in ("up", "down")]
        bf = [sem("up_stage"), sem("down_stage")]
        bx = [sem("up_cross"), sem("down_cross")]
        bb = sem("bias_stage")
        pool_c = sem("pool_c")

        passed = {nc.sync: sem("sp_passed"), nc.vector: sem("dve_passed"), nc.gpsimd: sem("pool_passed")}

        FILLN = 9 * DMA
        N_WX = 6

        block = ctx.enter_context(nc.Block())

        def each(eng, one):
            for i in (-1, 0, 1, 2):
                for s in steps(i, True):
                    one(s)
            with eng.Fori(3, B - 1) as i:
                for s in steps(i, False):
                    one(s)
            for i in (B - 1, B, B + 1):
                for s in steps(i, True):
                    one(s)

        def wait(eng, s, value):
            if isinstance(value, int) and value <= 0:
                return
            eng.wait_ge(s, value)

        def hold(eng, s, value):
            if isinstance(value, int):
                wait(eng, s, value)
            else:
                eng.wait_ge(s, value)
                eng.sem_inc(passed[eng], 1)

        @block.sync
        def _(sp):
            sp.dma_start(lora[:, :, :], lora_d).then_inc(lo_in, DMA)
            sp.dma_start(xT[:, :, :], xT_d[0, :, :].rearrange("(k p) t -> p k t", p=P))\
              .then_inc(xT_in, DMA)
            sp.dma_start(cs[:, :, :], cs_d).then_inc(cs_in, DMA)
            sp.dma_start(ident[:, :], ident_d).then_inc(c_in, DMA)
            sp.dma_start(mask[:, :], mask_d).then_inc(c_in, DMA)
            sp.dma_start(wo[:, :, :], wo_d.rearrange("(k p) c -> p k c", p=P)).then_inc(wx_in, DMA)
            sp.dma_start(w_x[:, :, :, :, :], wx_d).then_inc(wx_in, DMA)
            sp.dma_start(b_x[:, :, :], bx_d).then_inc(wx_in, DMA)
            sp.dma_start(tmp_x[:, :, :], bout_d.partition_broadcast(P)).then_inc(wx_in, DMA)
            for k in range(2):
                sp.dma_start(half_up[k][:, :, :],
                             wexpT_d[k * NPAIR:(k + 1) * NPAIR, :].rearrange("(b p) c -> p b c", p=P))\
                  .then_inc(wx_in, DMA)

            def one(step):
                kind, b, n = step
                if kind == "XTL":
                    hold(sp, done["QK"], 4 * b)
                    hold(sp, done["V"], 2 * b)
                    sp.dma_start(xT[:, :, :], xT_d[b, :, :].rearrange("(k p) t -> p k t", p=P))\
                      .then_inc(xT_in, DMA)
                elif kind == "XRES":
                    hold(sp, evac["WO"], 2 * b)
                    sp.dma_start(x_res[:, :, :], x_d[b, :, :].rearrange("(a p) c -> p a c", p=P))\
                      .then_inc(xres_in, DMA)
                elif kind == "ZL":
                    sp.wait_ge(done["UM"], NHT)
                    sp.dma_start(ga[:, 0:NHT * D].rearrange("p (b c) -> p b c", b=NHT),
                                 wcon_d.rearrange("(b p) c -> p b c", p=P)).then_inc(wz_in, DMA)
                elif kind == "QKW":
                    hold(sp, p3_done, 2 * b + n + 1)
                    sp.dma_start(qk_scr[b, n, :, :, :].rearrange("(e i) h t -> (i h) e t", i=8),
                                 parts[:, n, :, :, :].rearrange("p a e t -> p (a e) t"))\
                      .then_inc(qk_out, DMA)
                elif kind == "FILL":
                    hold(sp, qk_out, 2 * DMA * (b + 1))
                    hold(sp, st_done, NU * (b - 1) + UG * (n + 1))
                    hs = slice(GH * n, GH * n + GH)
                    for first, rows in ((0, 3), (3, 2), (5, 1)):
                        sp.dma_start(q_st[DH * first:DH * (first + rows), hs, :],
                                     qk_scr[b, 0, 0:DH * rows, hs, :]).then_inc(fill[n], DMA)
                    for row, (_, part) in enumerate(PRODUCTS):
                        sp.dma_start(k_st[DH * row:DH * (row + 1), hs, :],
                                     qk_scr[b, 1, DH * part:DH * (part + 1), hs, :])\
                          .then_inc(fill[n], DMA)
                elif kind == "MROW":
                    hold(sp, evac["MT"], NG * b + n + 1)
                    sp.dma_start(m_scr[b, n, :, :], m_row[:, :]).then_inc(mrow_out, DMA)
                    hold(sp, mrow_out, DMA * (NG * b + n + 1))
                    sp.dma_start(q_st[NK:NK + NPART, GH * n:GH * n + GH, :],
                                 m_scr[b, n, :, :].rearrange("(a h) t -> a h t", a=NPART))\
                      .then_inc(mrow_in, DMA)
                elif kind == "RAW":
                    hold(sp, o_evac, NG * b + n + 1)
                    sp.dma_start(o_scr[b, n, :, :], o_raw[:, :]).then_inc(raw_out, DMA)
                elif kind == "SMOC":
                    hold(sp, raw_out, DMA * (NG * b + 2 * n + 2))
                    hold(sp, done["WO"], 2 * b)
                    hold(sp, on_done, 2 * b + n)
                    both = o_scr[b, 2 * n:2 * n + 2, :, :].rearrange("g (h r) t -> (g h) r t", h=GH)
                    sp.dma_start(s_m[:, :], both[:, DH, :].rearrange("h (c t) -> h c t", c=8))\
                      .then_inc(sm_in, DMA)
                    sp.dma_start(o_c[:, n, :], both[:, 0:DH, :]).then_inc(oc_in, DMA)
                elif kind == "REC":
                    hold(sp, rcp_done, 2 * b + n + 1)
                    sp.dma_start(r_scr[b, n, :, :].rearrange("h (c t) -> (h c) t", c=8), r_m[:, :])\
                      .then_inc(rec_out, DMA)
                elif kind == "RB":
                    hold(sp, rec_out, DMA * (2 * b + n + 1))
                    hold(sp, on_done, 2 * b)
                    sp.dma_start(r_b[:, n, :],
                                 r_scr[b, n, :, :].unsqueeze(1).broadcast_to([8, DH, T]))\
                      .then_inc(rb_in, DMA)
                elif kind == "OUT":
                    hold(sp, lnd[1], b + 1)
                    sp.dma_start(out_d[b, :, :].rearrange("(a p) c -> p a c", p=P), y[:, :, :])\
                      .then_inc(out_sent, DMA)

            each(sp, one)
            sp.wait_ge(out_sent, DMA * B)

        @block.tensor
        def _(pe):
            pe.wait_ge(lo_in, DMA)
            for n in range(2 * KD):
                w, k = n // KD, n % KD
                if n:
                    pe.wait_ge(lora_add, n)
                pe.matmul(ps_m[:, 0:D], lora[:, w, k * P:(k + 1) * P], lora[:, 2 + w, :],
                          start=True, stop=True).then_inc(lora_mm, 1)
            pe.wait_ge(lora_add, 2 * KD)
            last = [None]

            def one(step):
                kind, b, n = step
                if kind in PER:
                    if last[0]:
                        k0, b0, n0 = last[0]
                        wait(pe, evac[k0], PER[k0] * b0 + n0 + 1)
                    last[0] = step
                if kind == "QK":
                    pe.wait_ge(xT_in, DMA * (b + 1))
                    for k in range(KD):
                        mm = pe.matmul(ps_m[:, :], wqk[:, k, n * P:(n + 1) * P], xT[:, k, :],
                                       start=(k == 0), stop=(k == KD - 1))
                    mm.then_inc(done["QK"], 1)
                elif kind == "V":
                    for j in range(2):
                        for k in range(KD):
                            mm = pe.matmul(ps_m[:, j * D:(j + 1) * D],
                                           xT[:, k, (2 * n + j) * P:(2 * n + j + 1) * P], wv[:, k, :],
                                           start=(k == 0), stop=(k == KD - 1))
                    mm.then_inc(done["V"], 1)
                elif kind == "S":
                    g, u = n // UG, n % UG
                    if u == 0:
                        pe.wait_ge(fill[g], FILLN * (b + 1))
                    wait(pe, max_done, NU * b + n)

                    def s_mm(off, qt, k0, k1, start):
                        h = hd
                        return pe.matmul(ps_s[:, off:off + (k1 - k0)],
                                         q_st[0:NK, h, pos(qt) * P:(pos(qt) + 1) * P],
                                         k_st[0:NK, h, k0:k1], start=start, stop=False,
                                         skip_group_check=True)

                    def s_mask(o, cols):
                        m = maskb[:, 0:P] if cols == P else \
                            maskb[:, :].rearrange("p (a c) -> p a c", a=2)
                        return pe.matmul(o, identb[:, :], m, start=False, stop=True,
                                         skip_group_check=True)

                    def pairs(bank):
                        return ps_s[:, bank * T:(bank + 1) * T].rearrange("p (a c) -> p a c", a=2)
                    if u < GH:
                        hd = GH * g + u
                        s_mm(0, 3, 0, T, True)
                        s_mask(ps_s[:, 2 * P:3 * P], P)
                        s_mm(T, 2, 0, 2 * P, True)
                        s_mm(T + 2 * P, 2, 3 * P, T, False)
                        s_mm(T + 3 * P, 0, 3 * P, T, False)
                        mm = s_mask(pairs(1)[:, :, P:2 * P], 2 * P)
                    else:
                        for j in range(GH):
                            hd = GH * g + j
                            s_mm(2 * P * j, 1, 0, P, j % 2 == 0)
                            s_mm(2 * P * j + P, 1, 3 * P, T, False)
                            if j % 2:
                                mm = s_mask(pairs(j // 2)[:, :, 0:P], 2 * P)
                    mm.then_inc(s_done, 1)
                elif kind == "ST":
                    g, u = n // UG, n % UG
                    if u == 0:
                        pe.wait_ge(mrow_in, DMA * (NG * b + g + 1))
                    wait(pe, exp_done, NU * b + n - 1)
                    dst = ps_t[:, n % 2, :]

                    def t_mm(off, h, kt, q0, q1, start):
                        return pe.matmul(dst[:, off:off + (q1 - q0)],
                                         k_st[0:NK + NPART, h, pos(kt) * P:(pos(kt) + 1) * P],
                                         q_st[0:NK + NPART, h, q0:q1], start=start, stop=True,
                                         skip_group_check=True)
                    if u < GH:
                        h = GH * g + u
                        t_mm(0, h, 0, 0, T, True)
                        t_mm(T, h, 3, 2 * P, 3 * P, True)
                        mm = t_mm(T + P, h, 1, 0, 3 * P, False)
                    else:
                        for j in range(GH):
                            mm = t_mm(2 * P * j, GH * g + j, 2, P, 3 * P, j % 2 == 0)
                    mm.then_inc(st_done, 1)
                elif kind == "MT":
                    pe.wait_ge(msplit, 4 * (NG * b + n + 1))
                    for t in range(NT):
                        mm = pe.transpose(ps_mb[0:NPART * GH, t * P:(t + 1) * P],
                                          m_part[:, t, :, :].rearrange("p a h -> p (a h)"),
                                          identb[:, :])
                    mm.then_inc(done["MT"], 1)
                elif kind == "PV":
                    g, c = n // 4, n % 4
                    if c == 0:
                        pe.wait_ge(vcopy, b + 1)
                        wait(pe, o_evac, NG * b + g)
                        pe.wait_ge(mask_done, NU * b + UG * g + GH)
                    if c == 3:
                        pe.wait_ge(mask_done, NU * b + UG * g + UG)
                    kt, q0, q1, off = [(0, 0, T, 0), (1, 0, 3 * P, T + P), (3, 2 * P, 3 * P, T),
                                       (2, P, 3 * P, None)][c]
                    for j in range(GH):
                        src = pT[:, g % 2, j, off:off + q1 - q0] if off is not None else \
                            pT[:, g % 2, GH, 2 * P * j:2 * P * (j + 1)]
                        mm = pe.matmul(ps_o[32 * j:32 * j + 32, q0:q1],
                                       v_aug[:, pos(kt), GH * g + j, :], src,
                                       start=(c == 0), stop=(c == 3), skip_group_check=True)
                    if c == 3:
                        mm.then_inc(pv_done, 1)
                elif kind == "WO":
                    pe.wait_ge(on_done, 2 * b + 2)
                    for j in range(2):
                        t = 2 * n + j
                        for k in range(KD):
                            mm = pe.matmul(ps_m[:, j * D:(j + 1) * D], o_c[:, k, t * P:(t + 1) * P],
                                           wo[:, k, :], start=(k == 0), stop=(k == KD - 1))
                    mm.then_inc(done["WO"], 1)
                elif kind == "XT":
                    pe.wait_ge(lnd[0], b + 1)
                    for t in range(NT):
                        mm = pe.transpose(ps_m[:, t * P:(t + 1) * P], x1[:, t, n * P:(n + 1) * P],
                                          ident[:, :])
                    mm.then_inc(done["XT"], 1)
                elif kind == "W1":
                    if n == 0:
                        pe.wait_ge(evac["XT"], 2 * b + 2)
                    for k in range(KD):
                        mm = pe.matmul(ps_m[:, :], w1[:, k, n * P:(n + 1) * P], x1T[:, k, :],
                                       start=(k == 0), stop=(k == KD - 1))
                    mm.then_inc(done["W1"], 1)
                elif kind == "W2":
                    if n == 0:
                        pe.wait_ge(gelu_done, b + 1)
                    for k in range(NHT):
                        mm = pe.matmul(ps_m[:, 0:D], gact[:, k, n * P:(n + 1) * P], w2[:, k, :],
                                       start=(k == 0), stop=(k == NHT - 1))
                    mm.then_inc(done["W2"], 1)
                elif kind == "UM":
                    if n == 0:
                        pe.wait_ge(bf[0], 6 * STAGES_IN + 1)
                        pe.wait_ge(wx_in, DMA * N_WX)
                    m_up = mat[0][STAGES_IN % 2][:, n * P:(n + 1) * P]
                    pe.matmul(ps_m[:, 0:D], m_up, tile_up[n], start=True, stop=True)
                    pe.matmul(ps_m[:, D:D + 1], m_up, b_x[:, 0, n:n + 1], start=False, stop=True,
                              skip_group_check=True).then_inc(done["UM"], 1)
                elif kind == "UT":
                    if n == 0:
                        pe.wait_ge(bx[0], 12 * 4)
                    k, half = n // 2, n % 2
                    for t in range(4):
                        mm = pe.transpose(ps_m[:, t * P:(t + 1) * P],
                                          tile_up[4 * half + t][:, k * P:(k + 1) * P], ident[:, :])
                    mm.then_inc(done["UT"], 1)
                elif kind == "DM":
                    if n == 0:
                        pe.wait_ge(bf[1], 6 * STAGES_IN + 1)
                        pe.wait_ge(bx[1], 12 * 4)
                    pe.matmul(ps_m[:, 0:D], mat[1][STAGES_IN % 2][:, n * P:(n + 1) * P], tile_dn[n],
                              start=True, stop=True).then_inc(done["DM"], 1)

            for i in (-1, 0, 1, 2):
                for s in steps(i, True):
                    one(s)
            with pe.Fori(3, B - 1) as i:
                last[0] = ("W1", i - 2, NHT - 1)
                for s in steps(i, False):
                    one(s)
            last[0] = ("W1", B - 3, NHT - 1)
            for i in (B - 1, B, B + 1):
                for s in steps(i, True):
                    one(s)

        @block.scalar
        def _(act):
            act.dma_start(wqk[:, :, :], wqk_d.rearrange("(k p) c -> p k c", p=P)).then_inc(w_in, DMA)
            act.dma_start(wv[:, :, :], wv_d.rearrange("(k p) c -> p k c", p=P)).then_inc(w_in, DMA)
            for half in range(2):
                act.dma_start(win[0][:, HID * half:HID * (half + 1)],
                              upin_d[0, HID * half:HID * (half + 1)].partition_broadcast(P))\
                   .then_inc(win_in[0][half], DMA)

            def one(step):
                kind, b, n = step
                if kind == "ST":
                    g, u = n // UG, n % UG
                    act.wait_ge(st_done, NU * b + n + 1)
                    if u == 0:
                        wait(act, pv_done, NG * b + g - 1)
                    act.activation(pT[:, g % 2, u, :], ps_t[:, n % 2, :], ACT.Exp, scale=SCALE)\
                       .then_inc(exp_done, 1)
                elif kind == "OE":
                    act.wait_ge(pv_done, NG * b + n + 1)
                    wait(act, raw_out, DMA * (NG * b + n))
                    act.activation(o_raw[:, :], ps_o[:, :], ACT.Copy).then_inc(o_evac, 1)
                elif kind == "V":
                    act.wait_ge(done["V"], 2 * b + n + 1)
                    wait(act, vcopy, b)
                    act.activation(v_new[:, 2 * n:2 * n + 2, :].rearrange("p a c -> p (a c)"),
                                   ps_m[:, :], ACT.Copy).then_inc(evac["V"], 1)
                elif kind == "VC":
                    wait(act, pv_done, NG * b)
                    act.wait_ge(evac["V"], 2 * b + 2)
                    act.wait_ge(pool_c, 1)
                    act.activation(v_aug[:, :, :, 0:DH],
                                   v_new[:, :, :].rearrange("p a (h d) -> p a h d", h=H), ACT.Copy)\
                       .then_inc(vcopy, 1)
                elif kind == "MT":
                    act.wait_ge(done["MT"], NG * b + n + 1)
                    wait(act, mrow_out, DMA * (NG * b + n))
                    act.activation(m_row[:, :], ps_mb[0:NPART * GH, 0:T], ACT.Copy)\
                       .then_inc(evac["MT"], 1)
                elif kind == "PART0":
                    act.wait_ge(rope_done, 2 * b + n + 1)
                    wait(act, qk_out, DMA * (2 * b - 1 + n))
                    act.activation(parts[:, n, 0, :, :], rot[:, :, :], ACT.Copy).then_inc(p1_done, 1)
                elif kind == "PART1":
                    act.wait_ge(r1_done, 2 * b + n + 1)
                    act.activation(parts[:, n, 1, :, :], rot[:, :, :], ACT.Copy).then_inc(p2_done, 1)
                elif kind == "XT":
                    act.wait_ge(done["XT"], 2 * b + n + 1)
                    wait(act, done["W1"], NHT * b)
                    act.activation(x1T[:, n, :], ps_m[:, :], ACT.Copy).then_inc(evac["XT"], 1)
                elif kind == "W1" and n % 2:
                    act.wait_ge(done["W1"], NHT * b + n + 1)
                    act.activation(gact[:, n, :], ps_m[:, :], ACT.Identity, bias=gbias[:, n:n + 1])\
                       .then_inc(evac["W1"], 1)
                elif kind == "GE":
                    act.wait_ge(evac["W1"], NHT * (b + 1))
                    act.activation(gact[:, :, :], gact[:, :, :], ACT.Gelu).then_inc(gelu_done, 1)
                elif kind == "BU" and n + 2 < 2 * STAGES_IN:
                    act.wait_ge(bf[0], 3 * n + 3)
                    act.dma_start(win[0][:, HID * (n % 2):HID * (n % 2 + 1)],
                                  upin_d[n // 2 + 1, HID * (n % 2):HID * (n % 2 + 1)]
                                  .partition_broadcast(P)).then_inc(win_in[0][n % 2], DMA)

            each(act, one)

        @block.vector
        def _(dve):
            dve.memset(k_st[96:P, :, :], 1.0).then_inc(c_ready, 1)
            dve.wait_ge(w_in, 2 * DMA)
            for n in range(2 * KD):
                dst = (wqk, wv)[n // KD][:, n % KD, 0:D]
                dve.wait_ge(lora_mm, n + 1)
                dve.scalar_tensor_tensor(out=dst, in0=ps_m[:, 0:D], scalar=LORA, in1=dst,
                                         op0=ALU.mult, op1=ALU.add).then_inc(lora_add, 1)
            dve.wait_ge(c_in, DMA * 2)
            dve.tensor_copy(identb[:, :], ident[:, :]).then_inc(c_ready, 1)
            dve.tensor_copy(maskb[:, :], mask[:, :]).then_inc(c_ready, 1)
            dve.tensor_copy(mat[0][0].rearrange("p (b c) -> p b c", b=NHT),
                            ident[:, :].unsqueeze(1).broadcast_to([P, NHT, P])).then_inc(bf[0], 1)
            dve.wait_ge(cs_in, DMA)

            def one(step):
                kind, b, n = step
                if kind == "S":
                    g, u = n // UG, n % UG
                    dve.wait_ge(s_done, NU * b + n + 1)
                    if u < GH:
                        for off, cols, qt in ((0, T, 3), (T, 3 * P, 2), (T + 3 * P, P, 0)):
                            ins = dve.tensor_reduce(m_raw[:, pos(qt), u:u + 1], ps_s[:, off:off + cols],
                                                    AX.X, ALU.max, negate=True)
                        ins.then_inc(max_done, 1)
                    else:
                        dve.tensor_reduce(m_raw[:, pos(1), :],
                                          ps_s[:, :].rearrange("p (h c) -> p h c", h=GH),
                                          AX.X, ALU.max, negate=True).then_inc(max_done, 1)
                        c0 = 4 * (NG * b + g)
                        dve.wait_ge(max_done, NU * b + n + 1)
                        wait(dve, done["MT"], NG * b + g)
                        dve.tensor_copy(m_part[:, :, 0, :], m_raw[:, :, :]).then_inc(msplit, 1)
                        dve.wait_ge(msplit, c0 + 1)
                        dve.tensor_tensor(m_res[:, :, :], m_raw[:, :, :], m_part[:, :, 0, :],
                                          ALU.subtract).then_inc(msplit, 1)
                        dve.wait_ge(msplit, c0 + 2)
                        dve.tensor_copy(m_part[:, :, 1, :], m_res[:, :, :]).then_inc(msplit, 1)
                        dve.wait_ge(msplit, c0 + 3)
                        dve.tensor_tensor(m_part[:, :, 2, :], m_res[:, :, :], m_part[:, :, 1, :],
                                          ALU.subtract).then_inc(msplit, 1)
                elif kind == "QK":
                    dve.wait_ge(done["QK"], 4 * b + n + 1)
                    if n % 2 == 0:
                        wait(dve, rope_done, 2 * b + n // 2 - 1)
                    a, c = ((0, 0), (1, 1)) if n % 2 == 0 else ((2, 1), (3, 0))
                    dve.tensor_tensor(rope_in[:, n // 2, a[0], :], ps_m[:, :], cs[:, a[1], :], ALU.mult)
                    dve.tensor_tensor(rope_in[:, n // 2, c[0], :], ps_m[:, :], cs[:, c[1], :], ALU.mult)\
                       .then_inc(evac["QK"], 1)
                elif kind == "RES1":
                    dve.wait_ge(p1_done, 2 * b + n + 1)
                    dve.tensor_tensor(rot[:, :, :], rot[:, :, :], parts[:, n, 0, :, :], ALU.subtract)\
                       .then_inc(r1_done, 1)
                elif kind == "PART2":
                    dve.wait_ge(p2_done, 2 * b + n + 1)
                    dve.tensor_tensor(parts[:, n, 2, :, :], rot[:, :, :], parts[:, n, 1, :, :],
                                      ALU.subtract).then_inc(p3_done, 1)
                elif kind == "RCP":
                    dve.wait_ge(sm_in, DMA * (2 * b + n + 1))
                    wait(dve, rec_out, DMA * (2 * b + n))
                    dve.reciprocal(r_m[:, :], s_m[:, :]).then_inc(rcp_done, 1)
                elif kind == "WO":
                    dve.wait_ge(done["WO"], 2 * b + n + 1)
                    if n == 0:
                        dve.wait_ge(xres_in, DMA * (b + 1))
                        wait(dve, x1b_done, b)
                        wait(dve, done["XT"], 2 * b)
                    dve.tensor_tensor(x1[:, 2 * n:2 * n + 2, :].rearrange("p a c -> p (a c)"),
                                      ps_m[:, :],
                                      x_res[:, 2 * n:2 * n + 2, :].rearrange("p a c -> p (a c)"),
                                      ALU.add).then_inc(evac["WO"], 1)
                elif kind == "W1" and n % 2 == 0:
                    dve.wait_ge(done["W1"], NHT * b + n + 1)
                    if n == 0:
                        wait(dve, done["W2"], NT * b)
                    dve.tensor_scalar(gact[:, n, :], ps_m[:, :], gbias[:, n:n + 1], None, ALU.add)\
                       .then_inc(evac["W1"], 1)
                elif kind == "W2":
                    dve.wait_ge(done["W2"], NT * b + n + 1)
                    if n == 0:
                        dve.wait_ge(x1b_done, b + 1)
                        wait(dve, out_sent, DMA * b)
                    dve.tensor_tensor(y[:, n, :], ps_m[:, 0:D], x1b[:, n, :], ALU.add)\
                       .then_inc(evac["W2"], 1)
                elif kind == "LNA":
                    src = (x1, y)[n]
                    dve.wait_ge((evac["WO"], evac["W2"])[n], (2, NT)[n] * (b + 1))
                    for t in range(NT):
                        ins = dve.bn_stats(stats[:, n, t, :], src[:, t, :])
                    ins.then_inc(st6[n], 1)
                    hold(dve, st6[n], b + 1)
                    for t in range(NT):
                        ins = dve.bn_aggr(mv[:, n, t, :], stats[:, n, t, :])
                    ins.then_inc(mv2[n], 1)
                    dve.wait_ge(mv2[n], b + 1)
                    dve.tensor_scalar(ve[:, n, :], mv[:, n, :, 1], EPS, None, ALU.add)\
                       .then_inc(ve1[n], 1)
                elif kind == "LNB":
                    src = (x1, y)[n]
                    dve.wait_ge(pw1[n], b + 1)
                    for t in range(NT):
                        ins = dve.tensor_scalar(src[:, t, :], src[:, t, :], mv[:, n, t, 0:1],
                                                rstd[:, n, t:t + 1], ALU.subtract, ALU.mult)
                    ins.then_inc(lnd[n], 1)
                elif kind == "BU":
                    butterfly_in(dve, 0, n, mat[0], win[0], win_in[0], bf[0], tmp_v)
                elif kind == "UM":
                    dve.wait_ge(done["UM"], n + 1)
                    dve.tensor_copy(b_x[:, 0, n:n + 1], ps_m[:, D:D + 1]).then_inc(bb, 1)
                    dve.tensor_copy(tile_up[n], ps_m[:, 0:D]).then_inc(evac["UM"], 1)
                    if n == 0:
                        dve.tensor_tensor(bias_out[:, :], tmp_x[:, 1, :], tmp_x[:, 0, :], ALU.add)\
                           .then_inc(c_ready, 1)
                        dve.wait_ge(c_ready, 4)
                elif kind == "UT":
                    k, half = n // 2, n % 2
                    dve.wait_ge(done["UT"], n + 1)
                    dve.tensor_copy(w1[:, k, T * half:T * (half + 1)], ps_m[:, :]).then_inc(evac["UT"], 1)
                elif kind == "DM":
                    dve.wait_ge(done["DM"], n + 1)
                    dve.tensor_copy(w2[:, n, :], ps_m[:, 0:D]).then_inc(evac["DM"], 1)
                elif kind in ("XU", "XD"):
                    k = int(kind == "XD")
                    if k and n == 0:
                        dve.wait_ge(wz_in, DMA)
                    elif n == 0:
                        dve.wait_ge(evac["UM"], NHT)
                    stage = n // 4 if k == 0 else STAGES_X - 1 - n // 4
                    cross(dve, (tile_up, tile_dn)[k], w_x[:, k, :, :, :], stage, n % 4, tmp_x, bx[k], 4 * n)
                elif kind == "XB":
                    dve.wait_ge(bb, NHT)
                    c = NHT
                    for st in range(STAGES_X):
                        pairs = b_x[:, 0, :].rearrange("p (n x k) -> p n x k", x=2, k=2 ** st)
                        for half in range(2):
                            for x in range(2):
                                w = w_x[:, 0, st, 2 * half + x, :].rearrange("p (n k) -> p n k", k=2 ** st)
                                o = b_t[:, half, :] if x == 0 else b_u[:, half, :]
                                dve.tensor_tensor(o.rearrange("p (n k) -> p n k", k=2 ** st),
                                                  pairs[:, :, x, :], w, ALU.mult).then_inc(bb, 1)
                                c += 1
                        dve.wait_ge(bb, c)
                        for half in range(2):
                            dve.tensor_tensor(pairs[:, :, half, :],
                                              b_t[:, half, :].rearrange("p (n k) -> p n k", k=2 ** st),
                                              b_u[:, half, :].rearrange("p (n k) -> p n k", k=2 ** st),
                                              ALU.add).then_inc(bb, 1)
                            c += 1
                        dve.wait_ge(bb, c)
                    dve.tensor_tensor(gbias[:, :], b_x[:, 1, :], b_x[:, 0, :], ALU.add).then_inc(c_ready, 1)
                    dve.wait_ge(c_ready, 5)

            each(dve, one)

        @block.gpsimd
        def _(pool):
            pool.memset(mhalf[:, :], -0.5)
            pool.memset(v_aug[:, :, :, :], 1.0).then_inc(pool_c, 1)
            for half in range(2):
                pool.dma_start(win[1][:, HID * half:HID * (half + 1)],
                               dnin_d[0, HID * half:HID * (half + 1)].partition_broadcast(P))\
                    .then_inc(win_in[1][half], DMA)
            pool.wait_ge(c_in, DMA * 2)
            pool.tensor_copy(mat[1][0].rearrange("p (b c) -> p b c", b=NHT),
                             ident[:, :].unsqueeze(1).broadcast_to([P, NHT, P])).then_inc(bf[1], 1)

            def one(step):
                kind, b, n = step
                if kind == "ST":
                    g, u = n // UG, n % UG
                    hold(pool, exp_done, NU * b + n + 1)
                    if u < GH:
                        v = pT[:, g % 2, u, 3 * P:6 * P].rearrange("p (a c) -> p a c", a=3)
                    else:
                        v = pT[:, g % 2, u, :].rearrange("p (a c) -> p a c", a=GH)[:, :, 0:P]
                    pool.affine_select(out=v, in_=v, compare_op=ALU.is_ge, fill=0.0, base=0,
                                       pattern=[[0, 3 if u < GH else GH], [1, P]],
                                       channel_multiplier=-1).then_inc(mask_done, 1)
                elif kind == "ROPE":
                    pool.wait_ge(evac["QK"], 4 * b + 2 * n + 2)
                    wait(pool, p3_done, 2 * b + n)
                    pool.tensor_tensor(rot[:, 0, :], rope_in[:, n, 0, :], rope_in[:, n, 2, :], ALU.subtract)
                    pool.tensor_tensor(rot[:, 1, :], rope_in[:, n, 1, :], rope_in[:, n, 3, :], ALU.add)\
                        .then_inc(rope_done, 1)
                elif kind == "ON":
                    pool.wait_ge(rb_in, DMA * (2 * b + n + 1))
                    pool.wait_ge(oc_in, DMA * (2 * b + n + 1))
                    pool.tensor_tensor(o_c[:, n, :], o_c[:, n, :], r_b[:, n, :], ALU.mult)\
                        .then_inc(on_done, 1)
                elif kind == "LNA":
                    pool.wait_ge(ve1[n], b + 1)
                    pool.tensor_tensor(rstd[:, n, :], ve[:, n, :], mhalf[:, :], ALU.pow)\
                        .then_inc(pw1[n], 1)
                elif kind == "LNB" and n == 0:
                    pool.wait_ge(lnd[0], b + 1)
                    pool.wait_ge(c_ready, 4)
                    wait(pool, evac["W2"], NT * b)
                    pool.tensor_tensor(x1b[:, :, :], x1[:, :, :],
                                       bias_out[:, :].unsqueeze(1).broadcast_to([P, NT, D]), ALU.add)\
                        .then_inc(x1b_done, 1)
                elif kind == "BD":
                    butterfly_in(pool, 1, n, mat[1], win[1], win_in[1], bf[1], tmp_p)
                    if n + 2 < 2 * STAGES_IN:
                        pool.dma_start(win[1][:, HID * (n % 2):HID * (n % 2 + 1)],
                                       dnin_d[n // 2 + 1, HID * (n % 2):HID * (n % 2 + 1)]
                                       .partition_broadcast(P)).then_inc(win_in[1][n % 2], DMA)

            each(pool, one)


def butterfly_in(eng, which, m, mat, w, w_in, count, tmp):
    s, half = m // 2, m % 2
    wv = w.rearrange("p (x k) -> p x k", x=4)
    t = tmp.rearrange("p (x k) -> p x k", x=2)
    size = 2 ** s if which == 0 else 2 ** (STAGES_IN - 1 - s)
    src = mat[s % 2].rearrange("p (n x k) -> p n x k", x=2, k=size)
    dst = mat[(s + 1) % 2].rearrange("p (n x k) -> p n x k", x=2, k=size)
    eng.wait_ge(w_in[half], DMA * (s + 1))
    eng.wait_ge(count, 1 + 3 * m)
    for x in range(2):
        eng.tensor_tensor(t[:, x, :].rearrange("p (n k) -> p n k", k=size), src[:, :, x, :],
                          wv[:, 2 * half + x, :].rearrange("p (n k) -> p n k", k=size),
                          ALU.mult).then_inc(count, 1)
    eng.wait_ge(count, 3 + 3 * m)
    eng.tensor_tensor(dst[:, :, half, :], t[:, 0, :].rearrange("p (n k) -> p n k", k=size),
                      t[:, 1, :].rearrange("p (n k) -> p n k", k=size), ALU.add).then_inc(count, 1)


def cross(eng, tiles, w, st, p, tmp, count, n):
    size = 2 ** st
    a = (p // size) * 2 * size + p % size
    first, second = tiles[a], tiles[a + size]
    if n:
        eng.wait_ge(count, n)
    eng.tensor_scalar(tmp[:, 0, :], second, w[:, st, 1, p:p + 1], None, ALU.mult).then_inc(count, 1)
    eng.tensor_scalar(tmp[:, 1, :], first, w[:, st, 2, p:p + 1], None, ALU.mult).then_inc(count, 1)
    eng.wait_ge(count, n + 2)
    eng.scalar_tensor_tensor(out=first, in0=first, scalar=w[:, st, 0, p:p + 1], in1=tmp[:, 0, :],
                             op0=ALU.mult, op1=ALU.add).then_inc(count, 1)
    eng.scalar_tensor_tensor(out=second, in0=second, scalar=w[:, st, 3, p:p + 1], in1=tmp[:, 1, :],
                             op0=ALU.mult, op1=ALU.add).then_inc(count, 1)


def kernel(**inputs):
    import numpy as np
    import concourse.bacc as bacc
    from concourse.bass_utils import run_bass_kernel_spmd as run

    def inp(name):
        return np.asarray(inputs["L0_" + name])

    x = inp("attn_query")
    order = np.concatenate([np.arange(P, T), np.arange(P)])
    xp = x[:, order, :]
    xT = np.zeros((B + 1, D, T), x.dtype)
    xT[:B] = xp.transpose(0, 2, 1)
    pair, head = np.meshgrid(np.arange(DH // 2), np.arange(H), indexing="ij")
    even = (head * DH + 2 * pair).ravel()
    eo = np.concatenate([even, even + 1])
    wqk = np.concatenate([inp("attn_wq")[:, eo], inp("attn_wk")[:, eo]], axis=1)

    def stage_weights(w, turned):
        w = w.reshape(w.shape[0], NPAIR, 4).transpose(0, 2, 1)
        return w[:, [0, 2, 1, 3]] if turned else w

    up, down = stage_weights(inp("ffn_up_weights"), False), stage_weights(inp("ffn_down_weights"), True)

    def across(w):
        return w[STAGES_IN:].reshape(STAGES_X, 4, 4, P).transpose(3, 0, 1, 2)

    i = np.arange(0, DH, 2, dtype=np.float32) / DH
    theta = order.astype(np.float32)[:, None] / np.float32(10000.0) ** i[None, :]
    theta = np.repeat(theta.T.astype(np.float64), H, axis=0)
    tri = np.where(np.arange(P)[None, :] > np.arange(P)[:, None], np.float32(-1e30), np.float32(0))

    arrays = {
        "xT": xT,
        "x": xp,
        "wqk": wqk,
        "wv": inp("attn_wv"),
        "lora": np.stack([inp("attn_Aq").T, inp("attn_Av").T, inp("attn_Bq")[:, eo], inp("attn_Bv")], axis=1),
        "wo": inp("attn_wo"),
        "wexpT": inp("ffn_W_exp").T,
        "upin": up[:STAGES_IN].reshape(STAGES_IN, 4 * NPAIR),
        "dnin": down[STAGES_IN - 1::-1].reshape(STAGES_IN, 4 * NPAIR),
        "wx": np.stack([across(up), across(down)], axis=1),
        "bx": np.stack([inp("ffn_b_exp").reshape(NHT, P).T, inp("ffn_up_bias").reshape(NHT, P).T], axis=1),
        "wcon": inp("ffn_W_con"),
        "bout": np.stack([inp("ffn_b_con"), inp("ffn_down_bias")]),
        "cs": np.stack([np.cos(theta), np.sin(theta)], axis=1).astype(np.float32),
        "ident": np.eye(P, dtype=np.float32),
        "mask": np.concatenate([tri, tri], axis=1),
    }
    nc = bacc.Bacc("TRN2", target_bir_lowering=False, num_devices=1)
    args = []
    for name in arrays:
        arrays[name] = np.ascontiguousarray(arrays[name])
        a = arrays[name]
        args.append(nc.dram_tensor(f"in_{name}", a.shape, mybir.dt.from_np(a.dtype), kind="ExternalInput").ap())
    args.append(nc.dram_tensor("out_0", (B, T, D), FP32, kind="ExternalOutput").ap())
    layer(nc, *args)
    r = run(nc, [{f"in_{k}": v for k, v in arrays.items()}], core_ids=[0])
    got = r.results[0]["out_0"]
    return got[:, np.argsort(order), :]
```

```python
import concourse.bass as bass
from concourse import mybir
from contextlib import ExitStack

FP32 = mybir.dt.float32
BF16 = mybir.dt.bfloat16
F32R = mybir.dt.float32r
ALU = mybir.AluOpType
ACT = mybir.ActivationFunctionType
AX = mybir.AxisListType

B, T, D = 16, 512, 256
H, DH = 16, 16
HID = 1024
P = 128
NT = T // P
KD = D // P
NHT = HID // P
GH = 4
NG = H // GH
UG = 5
NU = NG * UG
LEAD = 8
R = 8
NPART = 3
PRODUCTS = [(0, 0), (1, 0), (2, 0), (0, 1), (1, 1), (0, 2)]
NK = len(PRODUCTS) * DH
EPS = 1e-5
LORA = 4.0
SCALE = 0.25
STAGES_IN = 7
STAGES_X = 3
NPAIR = HID // 2
DMA = 16


def pos(tile):
    return (tile + NT - 1) % NT


def spread(when, kind, first, per):
    return [(when, first + k, kind, sum(per[:k]), c) for k, c in enumerate(per)]


SETUP_UNITS = (
    [(-1, 9, "BU", 0, 4)] +
    [(-1, 12 + t, "BU", 4 + t, 1) for t in range(4)] + [(0, t, "BU", 8 + t, 1) for t in range(6)] +
    [(-1, 6, "BD", 0, 5)] +
    [(0, t, "BD", 5 + t, 1) for t in range(9)] +
    [(0, 6, "EL", 0, 2)] + spread(0, "UM", 7, [2] * 4) + [(0, 11, "ZL", 0, 1)] +
    spread(0, "XU", 11, [1] * 8 + [2]) + [(1, 0, "XU", 10, 2), (1, 2, "XB", 0, 1)] +
    spread(1, "UT", 3, [1] * 4) + spread(1, "XD", 1, [1] * 12) + spread(1, "DM", 13, [4] * 2))




def steps(i, static):
    out = []

    def put(kind, b, n=0, top=B):
        if not static or 0 <= b < top:
            out.append((kind, b, n))

    def setup(when, kind, n=0):
        if static and i == when:
            out.append((kind, 0, n))

    first = {0: ("QK", i + 1, 0), 1: ("QK", i + 1, 1), 2: ("QK", i + 1, 2), 3: ("QK", i + 1, 3),
             4: ("W2", i - 2, 0), 5: ("W2", i - 2, 1), 6: ("W2", i - 2, 2), 8: ("W2", i - 2, 3),
             13: ("V", i + 1, 0), 11: ("WO", i - 1, 0), 12: ("WO", i - 1, 1),
             15: ("XT", i - 1, 0), 16: ("V", i + 1, 1), 17: ("W1", i - 1, 1),
             18: ("W1", i - 1, 3), 19: ("W1", i - 1, 5)}
    second = {12: ("MT", i, 3), 15: ("XT", i - 1, 1), 16: ("W1", i - 1, 0), 17: ("W1", i - 1, 2),
              18: ("W1", i - 1, 4), 19: ("W1", i - 1, 6)}
    third = {3: ("MT", i, 1), 7: ("MT", i, 2), 17: ("MT", i + 1, 0), 19: ("W1", i - 1, 7)}
    if static and i == B:
        first.update({5 + n: ("W2", i - 2, n) for n in range(NT)})
        del first[4]
    for t in range(NU):
        g, u = t // UG, t % UG
        if t == 0:
            put("OE", i - 1, 2)
            put("RAW", i - 1, 2)
        if t == 5:
            put("OE", i - 1, 3)
            put("VC", i)
            put("RAW", i - 1, 3)
            put("SMOC", i - 1, 1)
        if t == 10:
            put("OE", i, 0)
            put("RAW", i, 0)
        if t == 15:
            put("OE", i, 1)
            put("RAW", i, 1)
        if t == 14:
            put("LNB", i - 1, 0)
        put("ST", i, 2 * t)
        if t in first:
            put(*first[t])
            if first[t][0] == "W2":
                b, n = first[t][1:]
                if n + 1 < NT:
                    put("GHI", b, 2 * n + 2)
                    put("GLO", b, 2 * n + 2)
                put("W2E", b, n)
                if n + 1 < NT:
                    put("GHI", b, 2 * n + 3)
                    put("GLO", b, 2 * n + 3)
        if t == 3:
            for n in range(2):
                put("GHI", i - 2, n)
                put("GLO", i - 2, n)
        put("ST", i, 2 * t + 1)
        ahead = (i, 2 * (t + LEAD)) if t + LEAD < NU else (i + 1, 2 * (t + LEAD - NU))
        put("S", *ahead)
        if t in second:
            put(*second[t])
            if second[t][0] == "MT":
                put("MROW", second[t][1], second[t][2])
        if u >= 1:
            if g == 0:
                put("PV", i - 1, 4 * (NG - 1) + u - 1)
            else:
                put("PV", i, 4 * (g - 1) + u - 1)
        put("S", ahead[0], ahead[1] + 1)
        if t in third:
            put(*third[t])
            if third[t][0] == "MT":
                put("MROW", third[t][1], third[t][2])
        if t == 18:
            put("GE", i - 1, 0)
        if t == 0:
            put("GE", i - 2, 1)
        if t == 7:
            put("RB", i - 1, 1)
        for n in range(2):
            if t == 4 * n + 1:
                put("ROPE", i + 1, n)
            if t == 4 * n + 2:
                put("PART0", i + 1, n)
            if t == 3 * n + 3:
                put("RES1", i + 1, n)
            if t == 3 * n + 4:
                put("PART1", i + 1, n)
            if t == 4 * n + 4:
                put("PART2", i + 1, n)
                put("QKW", i + 1, n)
        if t == 8:
            put("XRES", i - 1)
        if t % UG == 3:
            put("FILL", *[(i, 3), (i + 1, 0), (i + 1, 1), (i + 1, 2)][g])
        if t == 6:
            put("RCP", i - 1, 1)
            put("REC", i - 1, 1)
        if t == 8:
            put("ON", i - 1, 1)
            put("LNS", i - 2, 2)
            put("LNS", i - 2, 3)
            put("LNA", i - 2, 1)
        if t == 10:
            put("LNB", i - 2, 1)
            put("OUT", i - 2)
        if t == 11:
            put("LNS", i - 1, 0)
        if t == 12:
            put("LNS", i - 1, 1)
            put("LNA", i - 1, 0)
        if t == 14:
            put("XTL", i + 2, 0, B + 1)
        if t == 16:
            put("SMOC", i, 0)
            put("BIAS", i - 1)
        if t == 17:
            put("RCP", i, 0)
            put("REC", i, 0)
            put("XHI", i + 2, 0, B + 1)
        if t == 18:
            put("XLO", i + 2, 0, B + 1)
        if t == 19:
            put("RB", i, 0)
        put("SEL", i, t)
        if t == 2:
            put("ON", i - 1, 0)
        for when, at, kind, n, count in SETUP_UNITS:
            if t == at:
                for k in range(n, n + count):
                    setup(when, kind, k)
    return out


ST_BANK = [m % 3 for m in range(2 * NU - 1)] + [1]
ST_BEFORE = [max(k - 2 * NU * (k >= m) for k in range(2 * NU) if ST_BANK[k] == ST_BANK[m])
             for m in range(2 * NU)]

PER = {"QK": 4, "V": 2, "MT": NG, "WO": 2, "XT": KD, "W1": NHT, "W2": NT, "UM": NHT, "UT": 4, "DM": NHT}
SHARED = [(kind, b - 5, n) for kind, b, n in steps(5, True) if kind in PER]
BANK = {(kind, n): k % 2 for k, (kind, _, n) in enumerate(SHARED)}
BANK.update({(kind, n): n % 2 for kind in ("UM", "UT", "DM") for n in range(PER[kind])})
BANK.update({("W2E", n): BANK["W2", n] for n in range(NT)})


def layer(nc, xT_d, x_d, wqk_d, wv_d, lora_d, wo_d, wexpT_d, upin_d, dnin_d, wx_d, bx_d, wcon_d,
          bout_d, cs_d, ident_d, mask_d, out_d):
    ctx = ExitStack()
    with ctx:
        def sb(name, shape, dt=FP32):
            return ctx.enter_context(nc.sbuf_tensor(name, shape, dt))

        def pb(name, shape, dt=FP32):
            return ctx.enter_context(nc.psum_tensor(name, shape, dt))

        def sem(name):
            return ctx.enter_context(nc.semaphore(name))

        q_st = sb("q_st", [P, H, T], BF16)
        k_st = sb("k_st", [P, H, T], BF16)
        pT = sb("pT", [P, 2, UG, 2 * T])
        xT_hi = sb("xT_hi", [P, KD, T], F32R)
        xT_lo = sb("xT_lo", [P, KD, T], F32R)
        cs = sb("cs", [P, 2, T])
        rope_in = sb("rope_in", [P, 4, T])
        rot = sb("rot", [P, 2, T])
        parts = sb("parts", [P, NPART, 2, T], BF16)
        v_new = sb("v_new", [P, NT, D])
        v_aug = sb("v_aug", [P, NT, H, 2 * DH])
        o_raw = sb("o_raw", [P, T])
        o_c = sb("o_c", [P, 2, T])
        r_b = sb("r_b", [P, 2, T])
        s_m = sb("s_m", [64, 64])
        r_m = sb("r_m", [64, 64])
        x_res = sb("x_res", [P, NT, D])
        x1T_hi = sb("x1T_hi", [P, KD, T], F32R)
        x1T_lo = sb("x1T_lo", [P, KD, T], F32R)
        gact = sb("gact", [P, NHT, T])
        y = sb("y", [P, NT, D])
        m_raw = sb("m_raw", [P, NT, GH])
        m_res = sb("m_res", [P, NT, GH])
        m_part = sb("m_part", [P, NT, NPART, GH], BF16)
        m_row = sb("m_row", [NPART * GH, T], BF16)
        wqk_hi = sb("wqk_hi", [P, KD, 4 * P], F32R)
        wqk_lo = sb("wqk_lo", [P, KD, 4 * P], F32R)
        wv_hi = sb("wv_hi", [P, KD, D], F32R)
        wv_lo = sb("wv_lo", [P, KD, D], F32R)
        w1_hi = sb("w1_hi", [P, KD, HID], F32R)
        w1_lo = sb("w1_lo", [P, KD, HID], F32R)
        wo = sb("wo", [P, KD, D])
        bias_out = sb("bias_out", [P, D])
        gbias = sb("gbias", [P, NHT])
        ident = sb("ident", [P, P])
        identb = sb("identb", [P, P], BF16)
        maskb = sb("maskb", [P, 2 * P], BF16)
        stats = sb("stats", [P, 2, NT, 6])
        mv = sb("mv", [P, 2, NT, 2])
        ve = sb("ve", [P, 2, NT])
        rstd = sb("rstd", [P, 2, NT])
        mhalf = sb("mhalf", [P, NT])
        w_x = sb("w_x", [P, 2, STAGES_X, 4, 4])
        b_x = sb("b_x", [P, 2, NHT])
        b_t = sb("b_t", [P, 2, 4])
        b_u = sb("b_u", [P, 2, 4])
        with ExitStack() as before_w2:
            win_dn = before_w2.enter_context(nc.sbuf_tensor("win_dn", [P, 2, HID], FP32))
            tmp_p = before_w2.enter_context(nc.sbuf_tensor("tmp_p", [P, HID], FP32))
        w2_hi = sb("w2_hi", [P, NHT, D], F32R)
        w2_lo = sb("w2_lo", [P, NHT, D], F32R)
        ga = gact[:, :, :].rearrange("p a c -> p (a c)")
        mat = [[ga[:, (2 * k + j) * HID:(2 * k + j + 1) * HID] for j in range(2)]
               for k in range(2)]
        wqk = pT[:, 0, 0, :].rearrange("p (k c) -> p k c", k=KD)
        wv = pT[:, 0, 1, 0:KD * D].rearrange("p (k c) -> p k c", k=KD)
        lora = pT[0:R, 0, 2, :].rearrange("p (a c) -> p a c", a=4)
        mask = pT[:, 0, 3, 0:2 * P]
        b_out = pT[:, 0, 3, T:2 * T].rearrange("p (a c) -> p a c", a=2)
        tmp_x = tmp_p[:, 0:2 * D].rearrange("p (a c) -> p a c", a=2)
        o_flat = o_c[:, :, :].rearrange("p a c -> p (a c)")
        y_flat = y[:, :, :].rearrange("p a c -> p (a c)")
        win = [[o_flat, y_flat], [win_dn[:, 0, :], win_dn[:, 1, :]]]
        tmp_v = x_res[:, :, :].rearrange("p a c -> p (a c)")
        half_up = (y, x_res)
        tile_up = [half_up[t // 4][:, t % 4, :] for t in range(NHT)]
        tile_dn = [ga[:, t * D:(t + 1) * D] for t in range(NHT)]

        xT = r_b
        ps_t = pb("ps_t", [P, 3, T])
        ps_s = pb("ps_s", [P, 2, T])
        ps_o = pb("ps_o", [P, T])
        ps_m = pb("ps_m", [P, 2, T])
        ps_lora = [ps_s[:, 0, 0:D], ps_o[:, 0:D], ps_m[:, 0, 0:D], ps_m[:, 1, 0:D]]

        qk_scr = nc.dram_tensor("qk_scr", (B, 2, NPART * DH, H, T), BF16, kind="Internal").ap()
        o_scr = nc.dram_tensor("o_scr", (B, NG, P, T), FP32, kind="Internal").ap()
        m_scr = nc.dram_tensor("m_scr", (B, NG, NPART * GH, T), BF16, kind="Internal").ap()
        r_scr = nc.dram_tensor("r_scr", (B, 2, 8, T), FP32, kind="Internal").ap()

        xT_in = sem("xT_in")
        xres_in = sem("xres_in")
        st_done, exp_done, mask_done = sem("st_done"), sem("exp_done"), sem("mask_done")
        s_done, max_done, msplit = sem("s_done"), sem("max_done"), sem("msplit")
        pv_done, o_evac, raw_out = sem("pv_done"), sem("o_evac"), sem("raw_out")
        sm_in, oc_in, rcp_done, rec_out = sem("sm_in"), sem("oc_in"), sem("rcp_done"), sem("rec_out")
        rb_in, on_done = sem("rb_in"), sem("on_done")
        xh_done, xl_done, x1h_done = sem("xT_hi_done"), sem("xT_lo_done"), sem("x1T_hi_done")
        mrow_out, mrow_in = sem("mrow_out"), sem("mrow_in")
        done = {k: sem(f"{k}_done") for k in PER}
        evac = {k: sem(f"{k}_evac") for k in PER}
        evac_w1 = [sem("W1_evac_act"), sem("W1_evac_dve")]
        rope_done, p1_done, p2_done = sem("rope_done"), sem("p1_done"), sem("p2_done")
        r1_done, p3_done, qk_out = sem("r1_done"), sem("p3_done"), sem("qk_out")
        fill = [sem(f"fill{g}") for g in range(NG)]
        vcopy = sem("vcopy")
        st6 = [sem("ln1_stats"), sem("ln2_stats")]
        mv2 = [sem("ln1_mv"), sem("ln2_mv")]
        ve1 = [sem("ln1_ve"), sem("ln2_ve")]
        pw1 = [sem("ln1_pow"), sem("ln2_pow")]
        lnd = [sem("ln1_done"), sem("ln2_done")]
        x1b_done, gelu_done, out_sent = sem("x1b_done"), sem("gelu_done"), sem("out_sent")
        c_in, wx_in, c_ready = sem("c_in"), sem("wx_in"), sem("c_ready")
        w_in = [sem("wqk_in"), sem("wv_in")]
        lo_in, cs_in, wz_in = sem("lora_in"), sem("cos_in"), sem("w_con_in")
        we_in = [sem(f"w_exp{k}_in") for k in range(2)]
        lora_mm, lora_add = sem("lora_mm"), sem("lora_add")
        win_in = [[sem(f"{w}_w{half}_in") for half in range(2)] for w in ("up", "down")]
        bf = [sem("up_stage"), sem("down_stage")]
        bx = [sem("up_cross"), sem("down_cross")]
        bt = [sem("up_products"), sem("down_products")]
        bb = sem("bias_stage")
        w_hi, w_lo = sem("w_hi"), sem("w_lo")
        w1h_done, w2h_done = sem("w1_hi_done"), sem("w2_hi_done")
        ghi_done, glo_done, w2_half = sem("gelu_hi_done"), sem("gelu_lo_done"), sem("w2_half_done")
        g_hi = x1T_hi[:, :, :].rearrange("p h (k c) -> p h k c", k=NHT // 2)
        g_lo = x1T_lo[:, :, :].rearrange("p h (k c) -> p h k c", k=NHT // 2)
        pool_c = sem("pool_c")

        passed = {nc.sync: sem("sp_passed"), nc.vector: sem("dve_passed"), nc.gpsimd: sem("pool_passed")}

        FILLN = 9 * DMA
        N_WX = 2

        block = ctx.enter_context(nc.Block())

        def each(eng, one):
            for i in (-1, 0, 1, 2):
                for s in steps(i, True):
                    one(s)
            with eng.Fori(3, B - 1) as i:
                for s in steps(i, False):
                    one(s)
            for i in (B - 1, B, B + 1):
                for s in steps(i, True):
                    one(s)

        def split_on(kind, b):
            first = {"PART2": 2, "XLO": 3}[kind]
            return nc.vector if isinstance(b, int) and b < first else nc.gpsimd

        def part2(eng, b, n):
            eng.wait_ge(p2_done, 2 * b + n + 1)
            eng.tensor_tensor(parts[:, 2, :, :], rot[:, :, :], parts[:, 1, :, :],
                              ALU.subtract).then_inc(p3_done, 1)

        def x_low(eng, b):
            eng.wait_ge(xh_done, b + 1)
            eng.tensor_tensor(xT_lo[:, :, :], xT[:, :, :], xT_hi[:, :, :].bitcast(FP32),
                              ALU.subtract).then_inc(xl_done, 1)

        def wait(eng, s, value):
            if isinstance(value, int) and value <= 0:
                return
            eng.wait_ge(s, value)

        def hold(eng, s, value):
            if isinstance(value, int):
                wait(eng, s, value)
            else:
                eng.wait_ge(s, value)
                eng.sem_inc(passed[eng], 1)

        @block.sync
        def _(sp):
            sp.dma_start(lora, lora_d).then_inc(lo_in, DMA)
            sp.dma_start(xT[:, :, :], xT_d[0, :, :].rearrange("(k p) t -> p k t", p=P))\
              .then_inc(xT_in, DMA)
            sp.dma_start(cs[:, :, :], cs_d).then_inc(cs_in, DMA)
            sp.dma_start(ident[:, :], ident_d).then_inc(c_in, DMA)
            sp.dma_start(mask, mask_d).then_inc(c_in, DMA)
            sp.dma_start(wo[:, :, :], wo_d.rearrange("(k p) c -> p k c", p=P)).then_inc(c_in, DMA)
            sp.dma_start(w_x[:, :, :, :, :], wx_d).then_inc(wx_in, DMA)
            sp.dma_start(b_x[:, :, :], bx_d).then_inc(wx_in, DMA)
            sp.dma_start(b_out, bout_d.partition_broadcast(P)).then_inc(c_in, DMA)

            def one(step):
                kind, b, n = step
                if kind == "XTL":
                    hold(sp, xl_done, b)
                    hold(sp, on_done, 2 * b - 4)
                    sp.dma_start(xT[:, :, :], xT_d[b, :, :].rearrange("(k p) t -> p k t", p=P))\
                      .then_inc(xT_in, DMA)
                elif kind == "XRES":
                    hold(sp, evac["W2"], NT * b)
                    if isinstance(b, int) and b == 0:
                        sp.wait_ge(done["UT"], 4)
                    sp.dma_start(x_res[:, :, :], x_d[b, :, :].rearrange("(a p) c -> p a c", p=P))\
                      .then_inc(xres_in, DMA)
                elif kind == "EL":
                    sp.wait_ge(bf[0], 6 * STAGES_IN + 1)
                    sp.dma_start(half_up[n][:, :, :],
                                 wexpT_d[n * NPAIR:(n + 1) * NPAIR, :].rearrange("(b p) c -> p b c", p=P))\
                      .then_inc(we_in[n], DMA)
                elif kind == "ZL":
                    sp.wait_ge(done["UM"], NHT)
                    sp.dma_start(ga[:, 0:NHT * D].rearrange("p (b c) -> p b c", b=NHT),
                                 wcon_d.rearrange("(b p) c -> p b c", p=P)).then_inc(wz_in, DMA)
                elif kind == "QKW":
                    hold(sp, p3_done, 2 * b + n + 1)
                    sp.dma_start(qk_scr[b, n, :, :, :].rearrange("(e i) h t -> (i h) e t", i=8),
                                 parts[:, :, :, :].rearrange("p a e t -> p (a e) t"))\
                      .then_inc(qk_out, DMA)
                elif kind == "FILL":
                    hold(sp, qk_out, 2 * DMA * (b + 1))
                    hold(sp, st_done, 2 * (NU * (b - 1) + UG * (n + 1)))
                    hs = slice(GH * n, GH * n + GH)
                    for first, rows in ((0, 3), (3, 2), (5, 1)):
                        sp.dma_start(q_st[DH * first:DH * (first + rows), hs, :],
                                     qk_scr[b, 0, 0:DH * rows, hs, :]).then_inc(fill[n], DMA)
                    for row, (_, part) in enumerate(PRODUCTS):
                        sp.dma_start(k_st[DH * row:DH * (row + 1), hs, :],
                                     qk_scr[b, 1, DH * part:DH * (part + 1), hs, :])\
                          .then_inc(fill[n], DMA)
                elif kind == "MROW":
                    hold(sp, evac["MT"], NG * b + n + 1)
                    sp.dma_start(m_scr[b, n, :, :], m_row[:, :]).then_inc(mrow_out, DMA)
                    hold(sp, mrow_out, DMA * (NG * b + n + 1))
                    sp.dma_start(q_st[NK:NK + NPART, GH * n:GH * n + GH, :],
                                 m_scr[b, n, :, :].rearrange("(a h) t -> a h t", a=NPART))\
                      .then_inc(mrow_in, DMA)
                elif kind == "RAW":
                    hold(sp, o_evac, NG * b + n + 1)
                    sp.dma_start(o_scr[b, n, :, :], o_raw[:, :]).then_inc(raw_out, DMA)
                elif kind == "SMOC":
                    hold(sp, raw_out, DMA * (NG * b + 2 * n + 2))
                    hold(sp, done["WO"], 2 * b)
                    hold(sp, on_done, 2 * b + n)
                    both = o_scr[b, 2 * n:2 * n + 2, :, :].rearrange("g (h r) t -> (g h) r t", h=GH)
                    sp.dma_start(s_m[:, :], both[:, DH, :].rearrange("h (c t) -> h c t", c=8))\
                      .then_inc(sm_in, DMA)
                    sp.dma_start(o_c[:, n, :], both[:, 0:DH, :]).then_inc(oc_in, DMA)
                elif kind == "REC":
                    hold(sp, rcp_done, 2 * b + n + 1)
                    sp.dma_start(r_scr[b, n, :, :].rearrange("h (c t) -> (h c) t", c=8), r_m[:, :])\
                      .then_inc(rec_out, DMA)
                elif kind == "RB":
                    hold(sp, rec_out, DMA * (2 * b + n + 1))
                    hold(sp, on_done, 2 * b)
                    if n == 0:
                        hold(sp, xl_done, min(b + 3, B + 1) if isinstance(b, int) else b + 3)
                    sp.dma_start(r_b[:, n, :],
                                 r_scr[b, n, :, :].unsqueeze(1).broadcast_to([8, DH, T]))\
                      .then_inc(rb_in, DMA)
                elif kind == "OUT":
                    hold(sp, lnd[1], b + 1)
                    sp.dma_start(out_d[b, :, :].rearrange("(a p) c -> p a c", p=P), y[:, :, :])\
                      .then_inc(out_sent, DMA)

            each(sp, one)
            sp.wait_ge(out_sent, DMA * B)

        @block.tensor
        def _(pe):
            pe.wait_ge(lo_in, DMA)
            for n in range(2 * KD):
                w, k = n // KD, n % KD
                pe.matmul(ps_lora[n], lora[:, w, k * P:(k + 1) * P], lora[:, 2 + w, :],
                          start=True, stop=True).then_inc(lora_mm, 1)
            pe.wait_ge(lora_add, 2 * KD)
            pe.wait_ge(w_lo, 2)

            def mm3(out, w, x):
                n = len(w[0])
                for j, (a, c) in enumerate(((0, 0), (0, 1), (1, 0))):
                    for k in range(n):
                        mm = pe.matmul(out, w[a][k], x[c][k], start=(j == 0 and k == 0),
                                       stop=(j == 2 and k == n - 1))
                return mm

            last = [None, None]

            def evacuated(kind, b, n):
                if kind == "W1":
                    wait(pe, evac_w1[n % 2], NHT // 2 * b + n // 2 + 1)
                else:
                    wait(pe, evac[kind], PER[kind] * b + n + 1)

            def one(step):
                kind, b, n = step
                pm = ps_m[:, BANK[kind, n], :] if (kind, n) in BANK else None
                if kind in PER:
                    if last[BANK[kind, n]]:
                        evacuated(*last[BANK[kind, n]])
                    last[BANK[kind, n]] = step
                if kind == "QK":
                    pe.wait_ge(xl_done, b + 1)
                    mm = mm3(pm,
                             [[w[:, k, n * P:(n + 1) * P] for k in range(KD)] for w in (wqk_hi, wqk_lo)],
                             [[x[:, k, :] for k in range(KD)] for x in (xT_hi, xT_lo)])
                    mm.then_inc(done["QK"], 1)
                elif kind == "V":
                    for j in range(2):
                        ts = slice((2 * n + j) * P, (2 * n + j + 1) * P)
                        mm = mm3(pm[:, j * D:(j + 1) * D],
                                 [[x[:, k, ts] for k in range(KD)] for x in (xT_hi, xT_lo)],
                                 [[w[:, k, :] for k in range(KD)] for w in (wv_hi, wv_lo)])
                    mm.then_inc(done["V"], 1)
                elif kind == "S":
                    g, u, half = n // 2 // UG, n // 2 % UG, n % 2
                    if u == 0 and half == 0:
                        pe.wait_ge(fill[g], FILLN * (b + 1))
                    wait(pe, max_done, 2 * NU * b + n - 1)

                    def s_mm(off, h, qt, k0, k1, start):
                        return pe.matmul(ps_s[:, half, off:off + (k1 - k0)],
                                         q_st[0:NK, h, pos(qt) * P:(pos(qt) + 1) * P],
                                         k_st[0:NK, h, k0:k1], start=start, stop=False,
                                         skip_group_check=True)

                    def s_mask(o, cols):
                        m = maskb[:, 0:P] if cols == P else \
                            maskb[:, :].rearrange("p (a c) -> p a c", a=2)
                        return pe.matmul(o, identb[:, :], m, start=False, stop=True,
                                         skip_group_check=True)

                    pairs = ps_s[:, half, :].rearrange("p (a c) -> p a c", a=2)
                    h = GH * g + u
                    if u < GH and half == 0:
                        s_mm(0, h, 3, 0, T, True)
                        mm = s_mask(ps_s[:, half, 2 * P:3 * P], P)
                    elif u < GH:
                        s_mm(0, h, 2, 0, 2 * P, True)
                        s_mm(2 * P, h, 2, 3 * P, T, False)
                        s_mm(3 * P, h, 0, 3 * P, T, False)
                        mm = s_mask(pairs[:, :, P:2 * P], 2 * P)
                    else:
                        for j in range(2):
                            s_mm(2 * P * j, GH * g + 2 * half + j, 1, 0, P, j == 0)
                            s_mm(2 * P * j + P, GH * g + 2 * half + j, 1, 3 * P, T, False)
                        mm = s_mask(pairs[:, :, 0:P], 2 * P)
                    mm.then_inc(s_done, 1)
                elif kind == "ST":
                    g, u, half = n // 2 // UG, n // 2 % UG, n % 2
                    if u == 0 and half == 0:
                        pe.wait_ge(mrow_in, DMA * (NG * b + g + 1))
                    wait(pe, exp_done, 2 * NU * b + ST_BEFORE[n] + 1)
                    dst = ps_t[:, ST_BANK[n], :]

                    def t_mm(off, h, kt, q0, q1, start):
                        return pe.matmul(dst[:, off:off + (q1 - q0)],
                                         k_st[0:NK + NPART, h, pos(kt) * P:(pos(kt) + 1) * P],
                                         q_st[0:NK + NPART, h, q0:q1], start=start, stop=True,
                                         skip_group_check=True)
                    if u < GH and half == 0:
                        mm = t_mm(0, GH * g + u, 0, 0, T, True)
                    elif u < GH:
                        t_mm(0, GH * g + u, 3, 2 * P, 3 * P, True)
                        mm = t_mm(P, GH * g + u, 1, 0, 3 * P, False)
                    else:
                        for j in range(2):
                            mm = t_mm(2 * P * j, GH * g + 2 * half + j, 2, P, 3 * P, j == 0)
                    mm.then_inc(st_done, 1)
                elif kind == "MT":
                    pe.wait_ge(msplit, 4 * (NG * b + n + 1))
                    for t in range(NT):
                        mm = pe.transpose(pm.bitcast(BF16)[0:NPART * GH, t * P:(t + 1) * P],
                                          m_part[:, t, :, :].rearrange("p a h -> p (a h)"),
                                          identb[:, :])
                    mm.then_inc(done["MT"], 1)
                elif kind == "PV":
                    g, c = n // 4, n % 4
                    if c == 0:
                        pe.wait_ge(vcopy, b + 1)
                        wait(pe, o_evac, NG * b + g)
                        pe.wait_ge(mask_done, NU * b + UG * g + GH)
                    if c == 3:
                        pe.wait_ge(mask_done, NU * b + UG * g + UG)
                    kt, q0, q1, off = [(0, 0, T, 0), (1, 0, 3 * P, T + P), (3, 2 * P, 3 * P, T),
                                       (2, P, 3 * P, None)][c]
                    for j in range(GH):
                        src = pT[:, g % 2, j, off:off + q1 - q0] if off is not None else \
                            pT[:, g % 2, GH, 2 * P * j:2 * P * (j + 1)]
                        mm = pe.matmul(ps_o[32 * j:32 * j + 32, q0:q1],
                                       v_aug[:, pos(kt), GH * g + j, :], src,
                                       start=(c == 0), stop=(c == 3), skip_group_check=True)
                    if c == 3:
                        mm.then_inc(pv_done, 1)
                elif kind == "WO":
                    pe.wait_ge(on_done, 2 * b + 2)
                    for j in range(2):
                        t = 2 * n + j
                        for k in range(KD):
                            mm = pe.matmul(pm[:, j * D:(j + 1) * D], o_c[:, k, t * P:(t + 1) * P],
                                           wo[:, k, :], start=(k == 0), stop=(k == KD - 1))
                    mm.then_inc(done["WO"], 1)
                elif kind == "XT":
                    pe.wait_ge(lnd[0], b + 1)
                    for t in range(NT):
                        mm = pe.transpose(pm[:, t * P:(t + 1) * P], x_res[:, t, n * P:(n + 1) * P],
                                          ident[:, :])
                    mm.then_inc(done["XT"], 1)
                elif kind == "W1":
                    if n == 0:
                        pe.wait_ge(evac["XT"], 2 * b + 2)
                    mm = mm3(pm,
                             [[w[:, k, n * P:(n + 1) * P] for k in range(KD)] for w in (w1_hi, w1_lo)],
                             [[x[:, k, :] for k in range(KD)] for x in (x1T_hi, x1T_lo)])
                    mm.then_inc(done["W1"], 1)
                elif kind == "W2":
                    for half in range(2):
                        pe.wait_ge(glo_done, NHT * b + 2 * n + half + 1)
                        for j, (a, c) in enumerate(((0, 0), (0, 1), (1, 0))):
                            for k in range(NHT // 2):
                                mm = pe.matmul(pm[:, 0:D], (g_hi, g_lo)[a][:, half, k, :],
                                               (w2_hi, w2_lo)[c][:, NHT // 2 * half + k, :],
                                               start=(half + j + k == 0),
                                               stop=(half == 1 and j == 2 and k == NHT // 2 - 1))
                        if half == 0:
                            mm.then_inc(w2_half, 1)
                    mm.then_inc(done["W2"], 1)
                elif kind == "UM":
                    if n == 0:
                        pe.wait_ge(bf[0], 6 * STAGES_IN + 1)
                        pe.wait_ge(wx_in, DMA * N_WX)
                    if n % 4 == 0:
                        pe.wait_ge(we_in[n // 4], DMA)
                    m_up = mat[0][STAGES_IN % 2][:, n * P:(n + 1) * P]
                    pe.matmul(pm[:, 0:D], m_up, tile_up[n], start=True, stop=True)
                    pe.matmul(pm[:, D:D + 1], m_up, b_x[:, 0, n:n + 1], start=False, stop=True,
                              skip_group_check=True).then_inc(done["UM"], 1)
                elif kind == "UT":
                    if n == 0:
                        pe.wait_ge(bx[0], 12 * 2)
                    k, half = n // 2, n % 2
                    for t in range(4):
                        mm = pe.transpose(pm[:, t * P:(t + 1) * P],
                                          tile_up[4 * half + t][:, k * P:(k + 1) * P], ident[:, :])
                    mm.then_inc(done["UT"], 1)
                elif kind == "DM":
                    if n == 0:
                        pe.wait_ge(bf[1], 6 * STAGES_IN + 1)
                        pe.wait_ge(bx[1], 12 * 2)
                    pe.matmul(pm[:, 0:D], mat[1][STAGES_IN % 2][:, n * P:(n + 1) * P], tile_dn[n],
                              start=True, stop=True).then_inc(done["DM"], 1)

            for i in (-1, 0, 1, 2):
                for s in steps(i, True):
                    one(s)
            with pe.Fori(3, B - 1) as i:
                for kind, b, n in SHARED[-2:]:
                    last[BANK[kind, n]] = (kind, b + i - 1, n)
                for s in steps(i, False):
                    one(s)
            for kind, b, n in SHARED[-2:]:
                last[BANK[kind, n]] = (kind, b + B - 2, n)
            for i in (B - 1, B, B + 1):
                for s in steps(i, True):
                    one(s)

        @block.scalar
        def _(act):
            act.dma_start(wqk, wqk_d.rearrange("(k p) c -> p k c", p=P)).then_inc(w_in[0], DMA)
            act.dma_start(wv, wv_d.rearrange("(k p) c -> p k c", p=P)).then_inc(w_in[1], DMA)
            for half in range(2):
                act.dma_start(win[0][half],
                              upin_d[0, HID * half:HID * (half + 1)].partition_broadcast(P))\
                   .then_inc(win_in[0][half], DMA)
            act.wait_ge(xT_in, DMA)
            act.activation(xT_hi[:, :, :], xT[:, :, :], ACT.Copy).then_inc(xh_done, 1)
            act.wait_ge(lora_add, KD)
            act.activation(wqk_hi[:, :, :], wqk, ACT.Copy).then_inc(w_hi, 1)
            act.wait_ge(lora_add, 2 * KD)
            act.activation(wv_hi[:, :, :], wv, ACT.Copy).then_inc(w_hi, 1)

            def one(step):
                kind, b, n = step
                pm = ps_m[:, BANK[kind, n], :] if (kind, n) in BANK else None
                if kind == "ST":
                    g, u, half = n // 2 // UG, n // 2 % UG, n % 2
                    act.wait_ge(st_done, 2 * NU * b + n + 1)
                    if u == 0 and half == 0:
                        wait(act, pv_done, NG * b + g - 1)
                    act.activation(pT[:, g % 2, u, half * T:(half + 1) * T], ps_t[:, ST_BANK[n], :],
                                   ACT.Exp, scale=SCALE).then_inc(exp_done, 1)
                elif kind == "OE":
                    act.wait_ge(pv_done, NG * b + n + 1)
                    wait(act, raw_out, DMA * (NG * b + n))
                    act.activation(o_raw[:, :], ps_o[:, :], ACT.Copy).then_inc(o_evac, 1)
                elif kind == "V":
                    act.wait_ge(done["V"], 2 * b + n + 1)
                    wait(act, vcopy, b)
                    act.activation(v_new[:, 2 * n:2 * n + 2, :].rearrange("p a c -> p (a c)"),
                                   pm, ACT.Copy).then_inc(evac["V"], 1)
                elif kind == "VC":
                    wait(act, pv_done, NG * b)
                    act.wait_ge(evac["V"], 2 * b + 2)
                    act.wait_ge(pool_c, 1)
                    act.activation(v_aug[:, :, :, 0:DH],
                                   v_new[:, :, :].rearrange("p a (h d) -> p a h d", h=H), ACT.Copy)\
                       .then_inc(vcopy, 1)
                elif kind == "MT":
                    act.wait_ge(done["MT"], NG * b + n + 1)
                    wait(act, mrow_out, DMA * (NG * b + n))
                    act.activation(m_row[:, :], pm.bitcast(BF16)[0:NPART * GH, 0:T], ACT.Copy)\
                       .then_inc(evac["MT"], 1)
                elif kind == "PART0":
                    act.wait_ge(rope_done, 2 * b + n + 1)
                    wait(act, qk_out, DMA * (2 * b + n))
                    act.activation(parts[:, 0, :, :], rot[:, :, :], ACT.Copy).then_inc(p1_done, 1)
                elif kind == "PART1":
                    act.wait_ge(r1_done, 2 * b + n + 1)
                    act.activation(parts[:, 1, :, :], rot[:, :, :], ACT.Copy).then_inc(p2_done, 1)
                elif kind == "XT":
                    act.wait_ge(done["XT"], 2 * b + n + 1)
                    wait(act, done["W2"], NT * b)
                    act.activation(x1T_hi[:, n, :], pm, ACT.Copy).then_inc(x1h_done, 1)
                elif kind == "UT":
                    k, half = n // 2, n % 2
                    act.wait_ge(done["UT"], n + 1)
                    act.activation(w1_hi[:, k, T * half:T * (half + 1)], pm, ACT.Copy)\
                       .then_inc(w1h_done, 1)
                elif kind == "UM":
                    act.wait_ge(done["UM"], n + 1)
                    act.activation(b_x[:, 0, n:n + 1], pm[:, D:D + 1], ACT.Copy).then_inc(bb, 1)
                    act.activation(tile_up[n], pm[:, 0:D], ACT.Copy).then_inc(evac["UM"], 1)
                elif kind == "DM":
                    act.wait_ge(done["DM"], n + 1)
                    act.activation(w2_hi[:, n, :], pm[:, 0:D], ACT.Copy).then_inc(w2h_done, 1)
                elif kind == "GHI":
                    tile, half = n // 2, n % 2
                    if tile:
                        act.wait_ge((w2_half, done["W2"])[half], NT * b + tile)
                    else:
                        act.wait_ge(gelu_done, 2 * b + half + 1)
                    act.activation(g_hi[:, half, :, :],
                                   gact[:, NHT // 2 * half:NHT // 2 * (half + 1), tile * P:(tile + 1) * P],
                                   ACT.Copy).then_inc(ghi_done, 1)
                elif kind in ("XU", "XD"):
                    k = int(kind == "XD")
                    first, second, st, p = pair((tile_up, tile_dn)[k], k, n)
                    if n:
                        act.wait_ge(bx[k], 2 * n)
                    elif k:
                        act.wait_ge(wz_in, DMA)
                        act.wait_ge(bx[0], 12 * 2)
                    else:
                        act.wait_ge(evac["UM"], NHT)
                        act.wait_ge(bf[1], 6 * STAGES_IN + 1)
                    for x, tile in enumerate((second, first)):
                        act.activation(tmp_x[:, x, :], tile, ACT.Copy,
                                       scale=w_x[:, k, st, 1 + x, p:p + 1]).then_inc(bt[k], 1)
                elif kind == "XHI":
                    act.wait_ge(xT_in, DMA * (b + 1))
                    act.wait_ge(done["QK"], 4 * b)
                    act.wait_ge(done["V"], 2 * b)
                    act.activation(xT_hi[:, :, :], xT[:, :, :], ACT.Copy).then_inc(xh_done, 1)
                elif kind == "W1" and n % 2 == 0:
                    act.wait_ge(done["W1"], NHT * b + n + 1)
                    act.activation(gact[:, n, :], pm, ACT.Identity, bias=gbias[:, n:n + 1])\
                       .then_inc(evac_w1[0], 1)
                elif kind == "GE":
                    for par in range(2):
                        act.wait_ge(evac_w1[par], NHT // 2 * b + NHT // 4 * (n + 1))
                    part = gact[:, NHT // 2 * n:NHT // 2 * (n + 1), :]
                    act.activation(part, part, ACT.Gelu).then_inc(gelu_done, 1)
                elif kind == "BU" and n + 2 < 2 * STAGES_IN:
                    act.wait_ge(bf[0], 3 * n + 3)
                    act.dma_start(win[0][n % 2],
                                  upin_d[n // 2 + 1, HID * (n % 2):HID * (n % 2 + 1)]
                                  .partition_broadcast(P)).then_inc(win_in[0][n % 2], DMA)

            each(act, one)

        @block.vector
        def _(dve):
            dve.memset(k_st[96:P, :, :], 1.0).then_inc(c_ready, 1)
            for n in range(2 * KD):
                dve.wait_ge(w_in[n // KD], DMA)
                dst = (wqk, wv)[n // KD][:, n % KD, 0:D]
                dve.wait_ge(lora_mm, n + 1)
                dve.scalar_tensor_tensor(out=dst, in0=ps_lora[n], scalar=LORA, in1=dst,
                                         op0=ALU.mult, op1=ALU.add).then_inc(lora_add, 1)
            dve.wait_ge(xh_done, 1)
            dve.tensor_tensor(xT_lo[:, :, :], xT[:, :, :], xT_hi[:, :, :].bitcast(FP32), ALU.subtract)\
               .then_inc(xl_done, 1)
            for n, (lo, w, hi) in enumerate(((wqk_lo, wqk, wqk_hi), (wv_lo, wv, wv_hi))):
                dve.wait_ge(w_hi, n + 1)
                dve.tensor_tensor(lo[:, :, :], w, hi[:, :, :].bitcast(FP32), ALU.subtract).then_inc(w_lo, 1)
            dve.wait_ge(c_in, DMA * 4)
            dve.tensor_tensor(bias_out[:, :], b_out[:, 1, :], b_out[:, 0, :], ALU.add).then_inc(c_ready, 1)
            dve.tensor_copy(identb[:, :], ident[:, :]).then_inc(c_ready, 1)
            dve.tensor_copy(maskb[:, :], mask).then_inc(c_ready, 1)
            dve.tensor_copy(mat[0][0].rearrange("p (b c) -> p b c", b=NHT),
                            ident[:, :].unsqueeze(1).broadcast_to([P, NHT, P])).then_inc(bf[0], 1)
            dve.wait_ge(cs_in, DMA)

            def one(step):
                kind, b, n = step
                pm = ps_m[:, BANK[kind, n], :] if (kind, n) in BANK else None
                if kind == "S":
                    g, u, half = n // 2 // UG, n // 2 % UG, n % 2
                    dve.wait_ge(s_done, 2 * NU * b + n + 1)
                    if u < GH:
                        for off, cols, qt in (((0, T, 3),), ((0, 3 * P, 2), (3 * P, P, 0)))[half]:
                            ins = dve.tensor_reduce(m_raw[:, pos(qt), u:u + 1], ps_s[:, half, off:off + cols],
                                                    AX.X, ALU.max, negate=True)
                    else:
                        ins = dve.tensor_reduce(m_raw[:, pos(1), 2 * half:2 * half + 2],
                                                ps_s[:, half, :].rearrange("p (h c) -> p h c", h=2),
                                                AX.X, ALU.max, negate=True)
                    ins.then_inc(max_done, 1)
                    if u == GH and half:
                        c0 = 4 * (NG * b + g)
                        dve.wait_ge(max_done, 2 * NU * b + n + 1)
                        wait(dve, done["MT"], NG * b + g)
                        dve.tensor_copy(m_part[:, :, 0, :], m_raw[:, :, :]).then_inc(msplit, 1)
                        dve.wait_ge(msplit, c0 + 1)
                        dve.tensor_tensor(m_res[:, :, :], m_raw[:, :, :], m_part[:, :, 0, :],
                                          ALU.subtract).then_inc(msplit, 1)
                        dve.wait_ge(msplit, c0 + 2)
                        dve.tensor_copy(m_part[:, :, 1, :], m_res[:, :, :]).then_inc(msplit, 1)
                        dve.wait_ge(msplit, c0 + 3)
                        dve.tensor_tensor(m_part[:, :, 2, :], m_res[:, :, :], m_part[:, :, 1, :],
                                          ALU.subtract).then_inc(msplit, 1)
                elif kind == "QK":
                    dve.wait_ge(done["QK"], 4 * b + n + 1)
                    if n % 2 == 0:
                        wait(dve, rope_done, 2 * b + n // 2)
                    a, c = ((0, 0), (1, 1)) if n % 2 == 0 else ((2, 1), (3, 0))
                    dve.tensor_tensor(rope_in[:, a[0], :], pm, cs[:, a[1], :], ALU.mult)
                    dve.tensor_tensor(rope_in[:, c[0], :], pm, cs[:, c[1], :], ALU.mult)\
                       .then_inc(evac["QK"], 1)
                elif kind == "RES1":
                    dve.wait_ge(p1_done, 2 * b + n + 1)
                    dve.tensor_tensor(rot[:, :, :], rot[:, :, :], parts[:, 0, :, :], ALU.subtract)\
                       .then_inc(r1_done, 1)
                elif kind == "XT":
                    dve.wait_ge(x1h_done, 2 * b + n + 1)
                    dve.tensor_tensor(x1T_lo[:, n, :], pm, x1T_hi[:, n, :].bitcast(FP32),
                                      ALU.subtract).then_inc(evac["XT"], 1)
                elif kind == "PART2" and split_on(kind, b) == nc.vector:
                    part2(dve, b, n)
                elif kind == "XLO" and split_on(kind, b) == nc.vector:
                    x_low(dve, b)
                elif kind == "RCP":
                    dve.wait_ge(sm_in, DMA * (2 * b + n + 1))
                    wait(dve, rec_out, DMA * (2 * b + n))
                    dve.reciprocal(r_m[:, :], s_m[:, :]).then_inc(rcp_done, 1)
                elif kind == "WO":
                    dve.wait_ge(done["WO"], 2 * b + n + 1)
                    if n == 0:
                        dve.wait_ge(xres_in, DMA * (b + 1))
                    rows = x_res[:, 2 * n:2 * n + 2, :].rearrange("p a c -> p (a c)")
                    dve.tensor_tensor(rows, pm, rows, ALU.add).then_inc(evac["WO"], 1)
                elif kind == "W1" and n % 2:
                    dve.wait_ge(done["W1"], NHT * b + n + 1)
                    dve.tensor_scalar(gact[:, n, :], pm, gbias[:, n:n + 1], None, ALU.add)\
                       .then_inc(evac_w1[1], 1)
                elif kind == "GLO":
                    tile, half = n // 2, n % 2
                    dve.wait_ge(ghi_done, NHT * b + n + 1)
                    dve.tensor_tensor(g_lo[:, half, :, :],
                                      gact[:, NHT // 2 * half:NHT // 2 * (half + 1),
                                           tile * P:(tile + 1) * P],
                                      g_hi[:, half, :, :].bitcast(FP32), ALU.subtract)\
                       .then_inc(glo_done, 1)
                elif kind == "DM":
                    dve.wait_ge(w2h_done, n + 1)
                    dve.tensor_tensor(w2_lo[:, n, :], pm[:, 0:D], w2_hi[:, n, :].bitcast(FP32),
                                      ALU.subtract).then_inc(evac["DM"], 1)
                elif kind == "W2E":
                    dve.wait_ge(done["W2"], NT * b + n + 1)
                    if n == 0:
                        dve.wait_ge(x1b_done, b + 1)
                        wait(dve, out_sent, DMA * b)
                    dve.tensor_tensor(y[:, n, :], pm[:, 0:D], x_res[:, n, :], ALU.add)\
                       .then_inc(evac["W2"], 1)
                elif kind == "LNS":
                    ln, half = n // 2, n % 2
                    src, k = ((x_res, "WO"), (y, "W2"))[ln]
                    dve.wait_ge(evac[k], PER[k] * b + PER[k] // 2 * (half + 1))
                    for t in (2 * half, 2 * half + 1):
                        ins = dve.bn_stats(stats[:, ln, t, :], src[:, t, :])
                    ins.then_inc(st6[ln], 1)
                elif kind == "LNA":
                    hold(dve, st6[n], 2 * b + 2)
                    for t in range(NT):
                        ins = dve.bn_aggr(mv[:, n, t, :], stats[:, n, t, :])
                    ins.then_inc(mv2[n], 1)
                    dve.wait_ge(mv2[n], b + 1)
                    dve.tensor_scalar(ve[:, n, :], mv[:, n, :, 1], EPS, None, ALU.add)\
                       .then_inc(ve1[n], 1)
                elif kind == "LNB":
                    src = (x_res, y)[n]
                    dve.wait_ge(pw1[n], b + 1)
                    for t in range(NT):
                        ins = dve.tensor_scalar(src[:, t, :], src[:, t, :], mv[:, n, t, 0:1],
                                                rstd[:, n, t:t + 1], ALU.subtract, ALU.mult)
                    ins.then_inc(lnd[n], 1)
                elif kind == "BU":
                    butterfly_in(dve, 0, n, mat[0], win[0], win_in[0], bf[0], tmp_v)
                elif kind == "UT":
                    k, half = n // 2, n % 2
                    cols = slice(T * half, T * (half + 1))
                    dve.wait_ge(w1h_done, n + 1)
                    dve.tensor_tensor(w1_lo[:, k, cols], pm, w1_hi[:, k, cols].bitcast(FP32),
                                      ALU.subtract).then_inc(evac["UT"], 1)
                elif kind in ("XU", "XD"):
                    k = int(kind == "XD")
                    first, second, st, p = pair((tile_up, tile_dn)[k], k, n)
                    dve.wait_ge(bt[k], 2 * (n + 1))
                    for x, tile in enumerate((first, second)):
                        dve.scalar_tensor_tensor(out=tile, in0=tile, scalar=w_x[:, k, st, 3 * x, p:p + 1],
                                                 in1=tmp_x[:, x, :], op0=ALU.mult, op1=ALU.add)\
                           .then_inc(bx[k], 1)
                elif kind == "XB":
                    dve.wait_ge(bb, NHT)
                    c = NHT
                    for st in range(STAGES_X):
                        pairs = b_x[:, 0, :].rearrange("p (n x k) -> p n x k", x=2, k=2 ** st)
                        for half in range(2):
                            for x in range(2):
                                w = w_x[:, 0, st, 2 * half + x, :].rearrange("p (n k) -> p n k", k=2 ** st)
                                o = b_t[:, half, :] if x == 0 else b_u[:, half, :]
                                dve.tensor_tensor(o.rearrange("p (n k) -> p n k", k=2 ** st),
                                                  pairs[:, :, x, :], w, ALU.mult).then_inc(bb, 1)
                                c += 1
                        dve.wait_ge(bb, c)
                        for half in range(2):
                            dve.tensor_tensor(pairs[:, :, half, :],
                                              b_t[:, half, :].rearrange("p (n k) -> p n k", k=2 ** st),
                                              b_u[:, half, :].rearrange("p (n k) -> p n k", k=2 ** st),
                                              ALU.add).then_inc(bb, 1)
                            c += 1
                        dve.wait_ge(bb, c)
                    dve.tensor_tensor(gbias[:, :], b_x[:, 1, :], b_x[:, 0, :], ALU.add).then_inc(c_ready, 1)
                    dve.wait_ge(c_ready, 5)

            each(dve, one)

        @block.gpsimd
        def _(pool):
            pool.memset(mhalf[:, :], -0.5)
            pool.memset(v_aug[:, :, :, :], 1.0).then_inc(pool_c, 1)
            for half in range(2):
                pool.dma_start(win[1][half],
                               dnin_d[0, HID * half:HID * (half + 1)].partition_broadcast(P))\
                    .then_inc(win_in[1][half], DMA)
            pool.wait_ge(c_in, DMA * 4)
            pool.tensor_copy(mat[1][0].rearrange("p (b c) -> p b c", b=NHT),
                             ident[:, :].unsqueeze(1).broadcast_to([P, NHT, P])).then_inc(bf[1], 1)

            def one(step):
                kind, b, n = step
                if kind == "SEL":
                    g, u = n // UG, n % UG
                    hold(pool, exp_done, 2 * (NU * b + n + 1))
                    if u < GH:
                        v = pT[:, g % 2, u, 3 * P:6 * P].rearrange("p (a c) -> p a c", a=3)
                    else:
                        v = pT[:, g % 2, u, :].rearrange("p (a c) -> p a c", a=GH)[:, :, 0:P]
                    pool.affine_select(out=v, in_=v, compare_op=ALU.is_ge, fill=0.0, base=0,
                                       pattern=[[0, 3 if u < GH else GH], [1, P]],
                                       channel_multiplier=-1).then_inc(mask_done, 1)
                elif kind == "PART2" and split_on(kind, b) == nc.gpsimd:
                    part2(pool, b, n)
                elif kind == "XLO" and split_on(kind, b) == nc.gpsimd:
                    x_low(pool, b)
                elif kind == "ROPE":
                    pool.wait_ge(evac["QK"], 4 * b + 2 * n + 2)
                    wait(pool, p3_done, 2 * b + n)
                    pool.tensor_tensor(rot[:, 0, :], rope_in[:, 0, :], rope_in[:, 2, :], ALU.subtract)
                    pool.tensor_tensor(rot[:, 1, :], rope_in[:, 1, :], rope_in[:, 3, :], ALU.add)\
                        .then_inc(rope_done, 1)
                elif kind == "ON":
                    pool.wait_ge(rb_in, DMA * (2 * b + n + 1))
                    pool.wait_ge(oc_in, DMA * (2 * b + n + 1))
                    pool.tensor_tensor(o_c[:, n, :], o_c[:, n, :], r_b[:, n, :], ALU.mult)\
                        .then_inc(on_done, 1)
                elif kind == "LNA":
                    pool.wait_ge(ve1[n], b + 1)
                    pool.tensor_tensor(rstd[:, n, :], ve[:, n, :], mhalf[:, :], ALU.pow)\
                        .then_inc(pw1[n], 1)
                elif kind == "BIAS":
                    pool.wait_ge(done["XT"], KD * (b + 1))
                    pool.wait_ge(c_ready, 4)
                    pool.tensor_tensor(x_res[:, :, :], x_res[:, :, :],
                                       bias_out[:, :].unsqueeze(1).broadcast_to([P, NT, D]), ALU.add)\
                        .then_inc(x1b_done, 1)
                elif kind == "BD":
                    butterfly_in(pool, 1, n, mat[1], win[1], win_in[1], bf[1], tmp_p)
                    if n + 2 < 2 * STAGES_IN:
                        pool.dma_start(win[1][n % 2],
                                       dnin_d[n // 2 + 1, HID * (n % 2):HID * (n % 2 + 1)]
                                       .partition_broadcast(P)).then_inc(win_in[1][n % 2], DMA)

            each(pool, one)


def butterfly_in(eng, which, m, mat, w, w_in, count, tmp):
    s, half = m // 2, m % 2
    wv = w[half].rearrange("p (x k) -> p x k", x=2)
    t = tmp.rearrange("p (x k) -> p x k", x=2)
    size = 2 ** s if which == 0 else 2 ** (STAGES_IN - 1 - s)
    src = mat[s % 2].rearrange("p (n x k) -> p n x k", x=2, k=size)
    dst = mat[(s + 1) % 2].rearrange("p (n x k) -> p n x k", x=2, k=size)
    eng.wait_ge(w_in[half], DMA * (s + 1))
    eng.wait_ge(count, 1 + 3 * m)
    for x in range(2):
        eng.tensor_tensor(t[:, x, :].rearrange("p (n k) -> p n k", k=size), src[:, :, x, :],
                          wv[:, x, :].rearrange("p (n k) -> p n k", k=size),
                          ALU.mult).then_inc(count, 1)
    eng.wait_ge(count, 3 + 3 * m)
    eng.tensor_tensor(dst[:, :, half, :], t[:, 0, :].rearrange("p (n k) -> p n k", k=size),
                      t[:, 1, :].rearrange("p (n k) -> p n k", k=size), ALU.add).then_inc(count, 1)


def pair(tiles, k, n):
    st, p = (n // 4, STAGES_X - 1 - n // 4)[k], n % 4
    size = 2 ** st
    a = (p // size) * 2 * size + p % size
    return tiles[a], tiles[a + size], st, p


def kernel(**inputs):
    import numpy as np
    import concourse.bacc as bacc
    from concourse.bass_utils import run_bass_kernel_spmd as run

    def inp(name):
        return np.asarray(inputs["L0_" + name])

    x = inp("attn_query")
    order = np.concatenate([np.arange(P, T), np.arange(P)])
    xp = x[:, order, :]
    xT = np.zeros((B + 1, D, T), x.dtype)
    xT[:B] = xp.transpose(0, 2, 1)
    pair, head = np.meshgrid(np.arange(DH // 2), np.arange(H), indexing="ij")
    even = (head * DH + 2 * pair).ravel()
    eo = np.concatenate([even, even + 1])
    wqk = np.concatenate([inp("attn_wq")[:, eo], inp("attn_wk")[:, eo]], axis=1)

    def stage_weights(w, turned):
        w = w.reshape(w.shape[0], NPAIR, 4).transpose(0, 2, 1)
        return w[:, [0, 2, 1, 3]] if turned else w

    up, down = stage_weights(inp("ffn_up_weights"), False), stage_weights(inp("ffn_down_weights"), True)

    def across(w):
        return w[STAGES_IN:].reshape(STAGES_X, 4, 4, P).transpose(3, 0, 1, 2)

    i = np.arange(0, DH, 2, dtype=np.float32) / DH
    theta = order.astype(np.float32)[:, None] / np.float32(10000.0) ** i[None, :]
    theta = np.repeat(theta.T.astype(np.float64), H, axis=0)
    tri = np.where(np.arange(P)[None, :] > np.arange(P)[:, None], np.float32(-1e30), np.float32(0))

    arrays = {
        "xT": xT,
        "x": xp,
        "wqk": wqk,
        "wv": inp("attn_wv"),
        "lora": np.stack([inp("attn_Aq").T, inp("attn_Av").T, inp("attn_Bq")[:, eo], inp("attn_Bv")], axis=1),
        "wo": inp("attn_wo"),
        "wexpT": inp("ffn_W_exp").T,
        "upin": up[:STAGES_IN].reshape(STAGES_IN, 4 * NPAIR),
        "dnin": down[STAGES_IN - 1::-1].reshape(STAGES_IN, 4 * NPAIR),
        "wx": np.stack([across(up), across(down)], axis=1),
        "bx": np.stack([inp("ffn_b_exp").reshape(NHT, P).T, inp("ffn_up_bias").reshape(NHT, P).T], axis=1),
        "wcon": inp("ffn_W_con"),
        "bout": np.stack([inp("ffn_b_con"), inp("ffn_down_bias")]),
        "cs": np.stack([np.cos(theta), np.sin(theta)], axis=1).astype(np.float32),
        "ident": np.eye(P, dtype=np.float32),
        "mask": np.concatenate([tri, tri], axis=1),
    }
    nc = bacc.Bacc("TRN2", target_bir_lowering=False, num_devices=1)
    args = []
    for name in arrays:
        arrays[name] = np.ascontiguousarray(arrays[name])
        a = arrays[name]
        args.append(nc.dram_tensor(f"in_{name}", a.shape, mybir.dt.from_np(a.dtype), kind="ExternalInput").ap())
    args.append(nc.dram_tensor("out_0", (B, T, D), FP32, kind="ExternalOutput").ap())
    layer(nc, *args)
    r = run(nc, [{f"in_{k}": v for k, v in arrays.items()}], core_ids=[0])
    got = r.results[0]["out_0"]
    return got[:, np.argsort(order), :]
```
